# Optimizing a Trainium2 kernel written in Bass

```python
import numpy as np
import jax
import jax.numpy as jnp

def _softmax(x, axis=-1):
    return jax.nn.softmax(x, axis=axis)

def _gelu(x):
    return jax.nn.gelu(x, approximate=True)

def _silu(x):
    return jax.nn.silu(x)

def _sigmoid(x):
    return jax.nn.sigmoid(x)

def _layernorm(x, axis=-1, eps=1e-05):
    m = jnp.mean(x, axis=axis, keepdims=True)
    v = jnp.var(x, axis=axis, keepdims=True)
    return (x - m) / jnp.sqrt(v + eps)

def _scatter_add(tgt, idx, src, axis=0):
    return tgt.at[idx].add(src)

def _segment_sum(src, seg, n):
    return jax.ops.segment_sum(src, seg, n)
kernel_name = 'mk_macaron_d1_jaxref_r8_381056'

def setup_inputs(seed: int=0):
    np.random.seed(seed)
    _w = jnp.asarray

    def _L0_attn_setup():
        import jax, jax.numpy as jnp
        import numpy as np
        import math
        NH, NKV, D = (32, 8, 128)

        def _alibi_slopes(n):
            cp2 = 2 ** math.floor(math.log2(n))
            base = 2.0 ** (-8.0 / cp2)
            slopes = base ** np.arange(1, cp2 + 1, dtype=np.float32)
            if cp2 != n:
                extra_base = 2.0 ** (-4.0 / cp2)
                extra = extra_base ** np.arange(1, 1 + 2 * (n - cp2), 2, dtype=np.float32)
                slopes = np.concatenate([slopes, extra])
            return slopes.astype(np.float32)
        key = jax.random.key(seed)
        k1, k2, k3 = jax.random.split(key, 3)
        B, S, H = (4, 128, 512)
        qkv_out = NH * D + 2 * NKV * D
        return {'hidden_states': jax.random.normal(k1, (B, S, H), jnp.float32) * 0.02, 'w_qkv': jax.random.normal(k2, (H, qkv_out), jnp.float32) * 0.02, 'w_o': jax.random.normal(k3, (NH * D, H), jnp.float32) * 0.02}
    _L0_attn_in = _L0_attn_setup()

    def _L0_ffn_setup():
        import jax, jax.numpy as jnp
        import numpy as np
        RMS_EPS = 1e-05
        key = jax.random.key(seed)
        k1, k2, k3, k4 = jax.random.split(key, 4)
        B, S, H, I = (1, 256, 512, 1792)
        x = jax.random.normal(k1, (B, S, H), dtype=jnp.float32)
        ln_w = jnp.ones((H,), dtype=jnp.float32)
        gate_w = jax.random.normal(k2, (I, H), dtype=jnp.float32) * 0.02
        up_w = jax.random.normal(k3, (I, H), dtype=jnp.float32) * 0.02
        down_w = jax.random.normal(k4, (H, I), dtype=jnp.float32) * 0.02
        return {'x': x, 'ln_w': ln_w, 'gate_w': gate_w, 'up_w': up_w, 'down_w': down_w}
    _L0_ffn_in = _L0_ffn_setup()
    _d = {'L0_attn_hidden_states': _L0_attn_in['hidden_states'], 'L0_attn_w_qkv': _L0_attn_in['w_qkv'], 'L0_attn_w_o': _L0_attn_in['w_o'], 'L0_ffn_ln_w': _L0_ffn_in['ln_w'], 'L0_ffn_gate_w': _L0_ffn_in['gate_w'], 'L0_ffn_up_w': _L0_ffn_in['up_w'], 'L0_ffn_down_w': _L0_ffn_in['down_w']}
    _x0 = _d['L0_attn_hidden_states']
    _d['L0_attn_hidden_states'] = jax.random.normal(jax.random.fold_in(jax.random.key(seed), 1), (2, 512, 512), dtype=_x0.dtype)
    del _x0
    return _d

def reference(L0_attn_hidden_states, L0_attn_w_qkv, L0_attn_w_o, L0_ffn_ln_w, L0_ffn_gate_w, L0_ffn_up_w, L0_ffn_down_w):

    def _L0_attn_ref(hidden_states, w_qkv, w_o):
        import jax, jax.numpy as jnp
        import numpy as np
        import math
        NH, NKV, D = (32, 8, 128)

        def _alibi_slopes(n):
            cp2 = 2 ** math.floor(math.log2(n))
            base = 2.0 ** (-8.0 / cp2)
            slopes = base ** np.arange(1, cp2 + 1, dtype=np.float32)
            if cp2 != n:
                extra_base = 2.0 ** (-4.0 / cp2)
                extra = extra_base ** np.arange(1, 1 + 2 * (n - cp2), 2, dtype=np.float32)
                slopes = np.concatenate([slopes, extra])
            return slopes.astype(np.float32)
        B, S, H = hidden_states.shape
        G = NH // NKV
        scale = D ** (-0.5)
        qkv = hidden_states @ w_qkv
        q = qkv[..., :NH * D].reshape(B, S, NKV, G, D)
        k = qkv[..., NH * D:NH * D + NKV * D].reshape(B, S, NKV, D)
        v = qkv[..., NH * D + NKV * D:].reshape(B, S, NKV, D)
        scores = jnp.einsum('bqhgd,bkhd->bhgqk', q, k) * scale
        slopes = jnp.asarray(_alibi_slopes(NH)).reshape(NKV, G)
        pos = jnp.arange(S)
        rel = pos[:, None] - pos[None, :]
        sqrt_dist = jnp.sqrt(jnp.maximum(rel, 0).astype(jnp.float32))
        bias = -slopes[:, :, None, None] * sqrt_dist
        bias = jnp.where(rel[None, None] >= 0, bias, -jnp.inf)
        attn = jax.nn.softmax(scores + bias[None], axis=-1)
        out = jnp.einsum('bhgqk,bkhd->bqhgd', attn, v).reshape(B, S, NH * D)
        return out @ w_o

    def _L0_ffn_ref(x, ln_w, gate_w, up_w, down_w):
        import jax, jax.numpy as jnp
        import numpy as np
        RMS_EPS = 1e-05
        var = jnp.mean(jnp.square(x), axis=-1, keepdims=True)
        nx = x * jax.lax.rsqrt(var + RMS_EPS) * ln_w
        g = jnp.einsum('bsh,ih->bsi', nx, gate_w)
        u = jnp.einsum('bsh,ih->bsi', nx, up_w)
        return jnp.einsum('bsi,hi->bsh', jax.nn.silu(g) * u, down_w)
    x = L0_attn_hidden_states
    x = x + 0.5 * _L0_ffn_ref(_layernorm(x, axis=-1), L0_ffn_ln_w, L0_ffn_gate_w, L0_ffn_up_w, L0_ffn_down_w)
    x = x + _L0_attn_ref(_layernorm(x, axis=-1), L0_attn_w_qkv, L0_attn_w_o)
    x = x + 0.5 * _L0_ffn_ref(_layernorm(x, axis=-1), L0_ffn_ln_w, L0_ffn_gate_w, L0_ffn_up_w, L0_ffn_down_w)
    return x

_drawn_inputs = setup_inputs


def setup_inputs(seed=0):
    import zlib

    import numpy as np

    out = dict(_drawn_inputs(seed))
    spreads = {'L0_ffn_ln_w': (1.0, 0.2)}
    factors = {}
    for name, (base, spread) in spreads.items():
        noise = np.random.default_rng([zlib.crc32(name.encode()), seed]).standard_normal(out[name].shape)
        drawn = base * np.exp(spread * noise) if base else spread * noise
        out[name] = jnp.asarray(drawn.astype(out[name].dtype))
    for name, factor in factors.items():
        out[name] = (out[name] * factor).astype(out[name].dtype)
    return out
```

```python
from contextlib import ExitStack

import concourse.bass as bass
from concourse import mybir

F32 = mybir.dt.float32
F32R = mybir.dt.float32r
ALU = mybir.AluOpType
ACT = mybir.ActivationFunctionType

P = 128
D = 512
KT = D // P
SEQ = 512
NB = 2
QT = SEQ // P
INNER = 1792
NC = INNER // P
NG = 8
GH = 4
EPS = 1e-5
SCALE = float(P) ** -0.5
MASKED = 1e37

NW = 6
NR = 7
Y_ORDER = (2, 3, 0, 1)
RAWQ = 5
UNITS = 16
ds = bass.ds


def macaron_kernel(nc, x_in, w_gu, w_d, ln_w, w_qkv, w_o, ident_in, dist_in, slope_in, qscale_in, out):
    ctx = ExitStack()
    with ctx:
        def sem(name):
            return ctx.enter_context(nc.semaphore(name))

        base = (nc.sbuf_base + 31) // 32 * 32
        arena_bytes = (nc.sbuf_bytes_remaining - 64) // 32 * 32
        ctx.enter_context(nc.sbuf_tensor("arena", [P, arena_bytes], mybir.dt.uint8))
        cursor = [base]

        def place(name, shape, dt, at=None):
            size = 4
            for n in shape[1:]:
                size *= n
            where = cursor[0] if at is None else at
            if at is None:
                cursor[0] += (size + 31) // 32 * 32
                assert cursor[0] <= base + arena_bytes, (name, cursor[0] - base, arena_bytes)
            return nc.alloc_sbuf_tensor_at(name, shape, dt, offset=where)

        x = place("x", [P, NB * QT, D], F32)
        n_hi = [place(f"n_hi{b}", [P, KT, SEQ], F32R) for b in range(NB)]
        n_lo = [place(f"n_lo{b}", [P, KT, SEQ], F32R) for b in range(NB)]
        ident = place("ident", [P, P], F32)
        dist = place("dist", [P, SEQ], F32)
        slopes = place("slopes", [P, NG * GH], F32)
        qscales = place("qscales", [P, NG * GH], F32)
        slope_now = place("slope_now", [P, GH], F32)
        lnw = place("lnw", [P, KT], F32)
        stat6 = place("stat6", [P, QT, 6], F32)
        moments = [place(f"moments{b}", [P, QT, 2], F32) for b in range(NB)]
        half_power = place("half_power", [P, QT], F32)
        rs = [place(f"rs{n}", [P, QT], F32) for n in range(6)]
        rstd_of = [place(f"rstd_of{b}", [P, QT], F32) for b in range(NB)]
        neg_max = place("neg_max", [P, 2], F32)
        row_sum = place("row_sum", [P, 2], F32)
        row_inv = place("row_inv", [P, 2], F32)
        xn = [place(f"xn{n}", [P, D], F32) for n in range(2)]
        xw = [place(f"xw{n}", [P, KT, P], F32) for n in range(2)]
        raw_gu = [place(f"raw_gu{p}", [P, 2 * KT * P], F32) for p in range(2)]
        raw_d = [place(f"raw_d{p}", [P, D], F32) for p in range(2)]
        raw_q = [place(f"raw_q{p}", [P, D], F32) for p in range(RAWQ)]
        wo_hi = [place(f"wo_hi{h}", [P, D], F32R) for h in range(GH)]
        wo_lo = [place(f"wo_lo{h}", [P, D], F32R) for h in range(GH)]

        w_at = cursor[0]
        gu_hi = [place(f"gu_hi{p}", [P, 2, KT, P], F32R) for p in range(2)]
        gu_lo = [place(f"gu_lo{p}", [P, 2, KT, P], F32R) for p in range(2)]
        d_hi = [place(f"d_hi{p}", [P, D], F32R) for p in range(2)]
        d_lo = [place(f"d_lo{p}", [P, D], F32R) for p in range(2)]
        chunk = 4 * KT * P
        wq_hi = [place(f"wq_hi{r}", [P, KT, P], F32R, w_at + 2 * r * chunk) for r in range(5)]
        wq_lo = [place(f"wq_lo{r}", [P, KT, P], F32R, w_at + (2 * r + 1) * chunk) for r in range(5)]
        wv = place("wv", [P, KT, 2, P], F32R, w_at + 10 * chunk)

        h_at = cursor[0]
        pt_hi = [place(f"pt_hi{p}", [P, QT, 2 * P], F32R) for p in range(2)]
        pt_lo = [place(f"pt_lo{p}", [P, QT, 2 * P], F32R) for p in range(2)]
        row = 4 * SEQ
        silu = [place(f"silu{p}", [P, SEQ], F32, h_at + p * row) for p in range(2)]
        hf = [place(f"hf{p}", [P, SEQ], F32, h_at + (2 + p) * row) for p in range(2)]
        h_hi = [place(f"h_hi{p}", [P, SEQ], F32R, h_at + (4 + p) * row) for p in range(2)]
        h_lo = [place(f"h_lo{p}", [P, SEQ], F32R, h_at + (6 + p) * row) for p in range(2)]

        q_hi = [place(f"q_hi{b}", [P, GH, SEQ], F32R) for b in range(NB)]
        q_lo = [place(f"q_lo{b}", [P, GH, SEQ], F32R) for b in range(NB)]
        k_hi = [place(f"k_hi{b}", [P, SEQ], F32R) for b in range(NB)]
        k_lo = [place(f"k_lo{b}", [P, SEQ], F32R) for b in range(NB)]
        v_hi = [place(f"v_hi{b}", [P, QT, P], F32R) for b in range(NB)]
        v_lo = [place(f"v_lo{b}", [P, QT, P], F32R) for b in range(NB)]
        v_part = place("v_part", [P, 2, P], F32)
        v_sum = place("v_sum", [P, 2, P], F32)
        scores = [place(f"scores{h}", [P, SEQ], F32) for h in range(2)]
        probs = [place(f"probs{h}", [P, SEQ], F32) for h in range(2)]
        o_hi = [place(f"o_hi{p}", [P, GH, P], F32R) for p in range(2)]
        o_lo = [place(f"o_lo{p}", [P, GH, P], F32R) for p in range(2)]

        bank = [ctx.enter_context(nc.psum_tensor(f"bank{n}", [P, 512], F32)) for n in range(8)]
        ffn_y = bank[0:4]
        ffn_g, ffn_u = [bank[4], bank[5]], [bank[6], bank[7]]
        s_bank, pt_bank, o_bank, y_bank = bank[0:2], bank[2:4], bank[5], bank[7]
        pj_bank = [bank[4], bank[6]]
        ln_bank = {(0, 0): bank[0:2], (0, 1): bank[0:2], (1, 0): [bank[4], bank[6]],
                   (1, 1): [bank[5], bank[7]], (2, 0): [bank[4], bank[6]], (2, 1): bank[0:2]}

        consts_in = sem("consts_in")
        x_in_sem = [sem(f"x_in{b}") for b in range(NB)]
        gu_in = [sem(f"gu_in{p}") for p in range(2)]
        d_in = [sem(f"d_in{p}") for p in range(2)]
        q_in = [sem(f"q_in{p}") for p in range(RAWQ)]
        out_written = sem("out_written")
        stat_done, moments_done, rstd_steps, rstd_done = (sem(n) for n in ("stat_done", "moments_done", "rstd_steps", "rstd_done"))
        xn_done, xn_turned, xn_weighted, n_hi_done, n_split = (sem(n) for n in ("xn_done", "xn_turned", "xn_weighted", "n_hi_done", "n_split"))
        gu_hi_done, gu_split, d_hi_done, d_split = (sem(n) for n in ("gu_hi_done", "gu_split", "d_hi_done", "d_split"))
        gu_done, silu_done, h_done, h_hi_done, h_split = (sem(n) for n in ("gu_done", "silu_done", "h_done", "h_hi_done", "h_split"))
        down_done, ffn_y_done, ffn_y_added = (sem(n) for n in ("down_done", "ffn_y_done", "ffn_y_added"))
        wq_hi_done, wq_split = (sem(n) for n in ("wq_hi_done", "wq_split"))
        pj_done, pj_hi_done, pj_read = (sem(n) for n in ("pj_done", "pj_hi_done", "pj_read"))
        v_part_done, v_hi_done, v_split = (sem(n) for n in ("v_part_done", "v_hi_done", "v_split"))
        slope_set, s_done, biased, exp_done, inv_done, p_ready = (sem(n) for n in ("slope_set", "s_done", "biased", "exp_done", "inv_done", "p_ready"))
        pt_done, pt_hi_done, pt_split = (sem(n) for n in ("pt_done", "pt_hi_done", "pt_split"))
        pv_done, o_hi_done, o_free = (sem(n) for n in ("pv_done", "o_hi_done", "o_free"))
        scores_seen, chunk_begun = (sem(n) for n in ("scores_seen", "chunk_begun"))
        y_done, y_free = (sem(n) for n in ("y_done", "y_free"))

        f = lambda t: t.bitcast(F32)

        def ln_tile(stage, b, i):
            return (stage * NB + b) * QT + i

        def unit(n):
            return n // 8, QT - 1 - n % 8 // 2, n % 2

        def n_pt(i):
            return (i + 2) // 2

        PT_BEFORE = [sum(n_pt(unit(m)[1]) for m in range(n)) for n in range(UNITS + 1)]
        FILL = {0: ([("proj", 0)], []), 1: ([("proj", 1)], []), 2: ([("out", 3)], [("proj", 2)]),
                3: ([("proj", 3)], []), 4: ([("out", 2)], [("proj", 4)]), 5: ([("proj", 5)], []),
                6: ([("out", 1)], []), 7: ([], [("proj", 6), ("out", 0)])}
        LAST_FILL = {0: ([("stats", 0)], []), 1: ([("tile", 0), ("tile", 1)], []), 2: ([("out", 3)], []),
                     3: ([("tile", 2), ("tile", 3)], []), 4: ([("out", 2)], []), 5: ([], []),
                     6: ([("out", 1)], []), 7: ([], [("out", 0)])}

        def fillers(g, n):
            last = isinstance(g, int) and g == NG - 1 and n >= 8
            return (LAST_FILL if last else FILL)[n % 8]

        block = ctx.enter_context(nc.Block())

        @block.sync
        def _(sp):
            x_rows = x_in.rearrange("(t p) d -> p t d", p=P)
            out_rows = out.rearrange("(t p) d -> p t d", p=P)

            def load_gu(c, parity, before):
                sp.wait_ge(gu_split, before)
                sp.dma_start(raw_gu[parity][:, :], w_gu[c]).then_inc(gu_in[parity], 16)

            def load_d(c, parity, before):
                sp.wait_ge(d_split, before)
                sp.dma_start(raw_d[parity][:, :], w_d[c]).then_inc(d_in[parity], 16)

            def load_ffn_first(stage):
                for c in range(2):
                    if stage == 0:
                        sp.dma_start(raw_gu[c][:, :], w_gu[c]).then_inc(gu_in[c], 16)
                        sp.dma_start(raw_d[c][:, :], w_d[c]).then_inc(d_in[c], 16)
                    else:
                        load_gu(c, c, 2 * NC * stage - 1 + c)
                        load_d(c, c, 2 * NC * stage - 1 + c)

            def load_ffn_rest(stage):
                for h in range(NB):
                    first = 2 if h == 0 else 0
                    at = (stage * NB + h) * NC
                    with sp.Fori(0, (NC - first) // 2) as k:
                        for p in range(2):
                            c = 2 * k + (first + p)
                            for load, src, dst, done, s in ((load_gu, w_gu, raw_gu, gu_split, gu_in),
                                                            (load_d, w_d, raw_d, d_split, d_in)):
                                sp.wait_ge(done, c + (at - 1))
                                sp.dma_start(dst[p][:, :], src[ds(c, 1)].rearrange("a p n -> (a p) n")).then_inc(s[p], 16)

            def load_group(g):
                for q in range(NW + GH):
                    if isinstance(g, int):
                        if 10 * g + q >= RAWQ:
                            sp.wait_ge(wq_split, 10 * g + q - RAWQ + 1)
                        src = w_qkv[NW * g + q] if q < NW else w_o[GH * g + q - NW]
                    else:
                        sp.wait_ge(wq_split, 10 * g + (q - RAWQ + 1))
                        src = w_qkv[ds(NW * g + q, 1)] if q < NW else w_o[ds(GH * g + (q - NW), 1)]
                        src = src.rearrange("a p n -> (a p) n")
                    sp.dma_start(raw_q[q % RAWQ][:, :], src).then_inc(q_in[q % RAWQ], 16)

            sp.dma_start(x[:, 0:QT, :], x_rows[:, 0:QT, :]).then_inc(x_in_sem[0], 16)
            for dst, src in ((ident, ident_in), (lnw, ln_w), (dist, dist_in), (slopes, slope_in), (qscales, qscale_in)):
                sp.dma_start(dst[:, :], src).then_inc(consts_in, 16)
            load_ffn_first(0)
            sp.dma_start(x[:, QT:, :], x_rows[:, QT:, :]).then_inc(x_in_sem[1], 16)
            load_ffn_rest(0)
            load_group(0)
            with sp.Fori(1, NG) as g:
                load_group(g)
            load_ffn_first(1)
            load_ffn_rest(1)
            for b in range(NB):
                for n, i in enumerate(Y_ORDER):
                    sp.wait_ge(ffn_y_added, (NB + b) * QT + n + 1)
                    t = b * QT + i
                    sp.dma_start(out_rows[:, t, :], x[:, t, :]).then_inc(out_written, 16)
            sp.wait_ge(out_written, 16 * NB * QT)

        @block.gpsimd
        def _(pool):
            steps = [0]

            def step(ins):
                steps[0] += 1
                ins.then_inc(rstd_steps, 1)
                pool.wait_ge(rstd_steps, steps[0])

            def rstd(stage, b):
                at = stage * NB + b
                pool.wait_ge(moments_done, (at + 1) * QT)
                var, result = moments[b][:, :, 1], rstd_of[b][:, :]
                step(pool.tensor_scalar(rs[0][:, :], var, 1.0, EPS, ALU.mult, ALU.add))
                if stage == 1:
                    pool.tensor_tensor(result, rs[0][:, :], half_power[:, :], ALU.pow).then_inc(rstd_done, 1)
                    return
                step(pool.tensor_tensor(rs[1][:, :], rs[0][:, :], half_power[:, :], ALU.pow))
                step(pool.tensor_tensor(rs[2][:, :], var, rs[1][:, :], ALU.mult))
                step(pool.tensor_tensor(rs[3][:, :], rs[2][:, :], rs[1][:, :], ALU.mult))
                step(pool.tensor_scalar(rs[4][:, :], rs[3][:, :], 1.0, EPS, ALU.mult, ALU.add))
                step(pool.tensor_tensor(rs[5][:, :], rs[4][:, :], half_power[:, :], ALU.pow))
                pool.tensor_tensor(result, rs[5][:, :], rs[1][:, :], ALU.mult).then_inc(rstd_done, 1)

            def gu_low(p, count):
                pool.wait_ge(gu_hi_done, count)
                pool.tensor_tensor(gu_lo[p][:, :, :, :], raw_gu[p][:, :], f(gu_hi[p][:, :, :, :]),
                                   ALU.subtract).then_inc(gu_split, 1)

            def ffn(stage):
                at = stage * NB * NC
                with pool.Fori(0, (2 * NC - 4) // 2) as k:
                    for p in range(2):
                        gu_low(p, 2 * k + (at + 2 + p + 1))
                if stage == 0:
                    rstd(1, 0)
                for p in range(2):
                    gu_low(p, at + 2 * NC - 2 + p + 1)

            def split_group(g, prev):
                for q in range(NW + GH):
                    load_no = 2 * g + (q // RAWQ + 1)
                    pool.wait_ge(q_in[q % RAWQ], 16 * load_no)
                    if prev is None:
                        if q == 0:
                            pool.wait_ge(gu_done, 2 * NC)
                        if q == 4:
                            pool.wait_ge(down_done, 2 * NC)
                    else:
                        done, count = ((pj_done, 2 * NR * prev + (NR + q + 1)) if q < NW - 1 else
                                       (pj_done, 2 * NR * prev + 2 * NR) if q == NW - 1 else
                                       (y_done, 2 * QT * prev + 2 * QT))
                        pool.wait_ge(done, count)
                        pool.sem_inc(chunk_begun, 1)
                    raw = raw_q[q % RAWQ]
                    if q < NW - 1:
                        hi, lo, src = wq_hi[q][:, :, :], wq_lo[q][:, :, :], raw[:, :].rearrange("p (k n) -> p k n", k=KT)
                    elif q == NW - 1:
                        hi, lo, src = wv[:, :, 0, :], wv[:, :, 1, :], raw[:, :].rearrange("p (k n) -> p k n", k=KT)
                    else:
                        hi, lo, src = wo_hi[q - NW][:, :], wo_lo[q - NW][:, :], raw[:, :]
                    pool.tensor_scalar(hi, src, 1.0, 0.0, ALU.mult, ALU.add).then_inc(wq_hi_done, 1)
                    pool.wait_ge(wq_hi_done, 10 * g + (q + 1))
                    pool.tensor_tensor(lo, src, f(hi), ALU.subtract).then_inc(wq_split, 1)
                    if prev is None and q == 3:
                        rstd(1, 1)

            pool.memset(half_power[:, :], -0.5).then_inc(rstd_steps, 1)
            steps[0] = 1
            pool.wait_ge(rstd_steps, 1)
            rstd(0, 0)
            gu_low(0, 1)
            rstd(0, 1)
            gu_low(1, 2)
            ffn(0)
            split_group(0, None)
            with pool.Fori(0, NG - 1) as g:
                split_group(g + 1, g)
            rstd(2, 0)
            gu_low(0, 2 * NC + 1)
            gu_low(1, 2 * NC + 2)
            rstd(2, 1)
            ffn(1)

        @block.scalar
        def _(act):
            def n_high(stage, b, i):
                tile = ln_tile(stage, b, i)
                if stage == 1:
                    act.wait_ge(xn_turned, tile + 1)
                    src = ln_bank[stage, b][i % 2][:, :].rearrange("p (k n) -> p k n", k=KT)
                else:
                    act.wait_ge(xn_weighted, (stage // 2 * NB + b) * QT + i + 1)
                    src = xw[i % 2][:, :, :]
                act.copy(n_hi[b][:, :, i * P:(i + 1) * P], src).then_inc(n_hi_done, 1)

            def gu_high(p, landed, count):
                act.wait_ge(gu_in[p], landed)
                if not isinstance(count, int) or count >= 2:
                    act.wait_ge(gu_done, count - 1)
                act.copy(gu_hi[p][:, :, :, :], raw_gu[p][:, :]).then_inc(gu_hi_done, 1)

            def d_high(p, landed, count):
                act.wait_ge(d_in[p], landed)
                if not isinstance(count, int) or count >= 2:
                    act.wait_ge(down_done, count - 1)
                act.copy(d_hi[p][:, :], raw_d[p][:, :]).then_inc(d_hi_done, 1)

            def chunk(p, G, half_G, more_gu, more_d):
                act.wait_ge(gu_done, G + 1)
                act.activation(silu[p][:, :], ffn_g[p][:, :], ACT.Silu).then_inc(silu_done, 1)
                if more_gu:
                    gu_high(p, 16 * (half_G + 2), G + 2)
                act.wait_ge(h_done, G + 1)
                if not isinstance(G, int) or G >= 2:
                    act.wait_ge(down_done, G - 1)
                act.copy(h_hi[p][:, :], hf[p][:, :]).then_inc(h_hi_done, 1)
                if more_d:
                    d_high(1 - p, 16 * (half_G + p + 1), G + 1)

            def ffn(stage, b, between):
                at = (stage * NB + b) * NC
                for c in range(2):
                    chunk(c, at + c, at // 2, True, True)
                    between(c)
                with act.Fori(0, (NC - 4) // 2) as k:
                    for p in range(2):
                        chunk(p, 2 * k + (at + 2 + p), k + (at // 2 + 1), True, True)
                for c in range(NC - 2, NC):
                    chunk(c % 2, at + c, (at + c) // 2, b == 0, b == 0 or c == NC - 2)

            def ffn_start(stage):
                at = stage * NB * NC
                if stage:
                    act.wait_ge(pj_done, NG * NB * NR)
                gu_high(0, 16 * (at // 2 + 1), at)
                d_high(0, 16 * (at // 2 + 1), at)
                gu_high(1, 16 * (at // 2 + 1), at + 1)

            def ffn_both(stage):
                for i in range(2):
                    n_high(2 * stage, 1, i)
                ffn(stage, 0, lambda c: [n_high(2 * stage, 1, i) for i in (2, 3) if c == 0])
                ffn(stage, 1, lambda c: None)

            def project(g, b, r):
                R = 2 * NR * g + (NR * b + r)
                src = pj_bank[(b * NR + r) % 2]
                act.wait_ge(pj_done, R + 1)
                if r == 0:
                    act.copy(k_hi[b][:, :], src[:, :]).then_inc(pj_hi_done, 1)
                elif r < NW - 1:
                    scale = qscales[:, ds(GH * g + (r - 1), 1)] if not isinstance(g, int) else qscales[:, GH * g + r - 1:GH * g + r]
                    act.activation(q_hi[b][:, r - 1, :], src[:, :], ACT.Copy, scale=scale).then_inc(pj_hi_done, 1)
                else:
                    j = 2 * (r - NW + 1)
                    V = 2 * NB * g + (2 * b + r - NW + 1)
                    halves = src[:, :].rearrange("p (j a n) -> p j a n", j=2, a=2)
                    act.copy(v_part[:, :, :], halves[:, :, 1, :]).then_inc(v_part_done, 1)
                    act.wait_ge(pj_read, R + 1)
                    act.copy(v_hi[b][:, j:j + 2, :], v_sum[:, :, :]).then_inc(v_hi_done, 1)

            def fill(g, n, what):
                kind, arg = what
                b = n // 8
                if kind == "proj":
                    project(*((g, 1) if b == 0 else (g + 1, 0)), arg)
                if kind == "tile":
                    n_high(2, 0, arg)

            def exps(u):
                for h in range(2):
                    act.wait_ge(biased, 2 * u + (h + 1))
                    w = widths[h]
                    act.activation(probs[h][:, 0:w], scores[h][:, 0:w], ACT.Exp, bias=neg_max[:, h:h + 1],
                                   scale=-1.0, accum_out=row_sum[:, h:h + 1]).then_inc(exp_done, 1)

            widths = [0, 0]

            def slot(g, n):
                b, i, hp = unit(n)
                par = n % 2
                u = UNITS * g + n
                a_fill, b_fill = fillers(g, n)
                for m in range(n_pt(i)):
                    E = PT_BEFORE[UNITS] * g + (PT_BEFORE[n] + m + 1)
                    w = min(2, i + 1 - 2 * m) * 2 * P
                    act.wait_ge(pt_done, E)
                    act.copy(pt_hi[par][:, 2 * m:2 * m + w // (2 * P), :],
                             pt_bank[m][:, 0:w]).then_inc(pt_hi_done, 1)
                if not (isinstance(g, int) and g == NG - 1 and n == UNITS - 1):
                    widths[:] = [(unit((n + 1) % UNITS)[1] + 1) * P] * 2
                    exps(u + 1)
                for what in a_fill:
                    fill(g, n, what)
                act.wait_ge(pv_done, u + 1)
                act.copy(o_hi[i % 2][:, 2 * hp:2 * hp + 2, :], o_bank[:, 0:2 * P]).then_inc(o_hi_done, 1)
                for what in b_fill:
                    fill(g, n, what)

            act.wait_ge(consts_in, 16 * 5)
            ffn_start(0)
            for i in range(QT):
                n_high(0, 0, i)
            ffn_both(0)
            for i in range(QT):
                n_high(1, 0, i)
            for r in range(5):
                project(0, 0, r)
            n_high(1, 1, 0)
            n_high(1, 1, 1)
            project(0, 0, 5)
            n_high(1, 1, 2)
            n_high(1, 1, 3)
            project(0, 0, 6)
            widths[:] = [SEQ, SEQ]
            exps(0)
            with act.Fori(0, NG - 1) as g:
                for n in range(UNITS):
                    slot(g, n)
            for n in range(UNITS):
                slot(NG - 1, n)
            ffn_start(1)
            ffn_both(1)

        @block.vector
        def _(dve):
            def stats(stage, b):
                at = stage * NB + b
                if stage == 0:
                    dve.wait_ge(x_in_sem[b], 16)
                elif stage == 1:
                    dve.wait_ge(ffn_y_added, (b + 1) * QT)
                else:
                    dve.wait_ge(y_free, 1 + QT * (NB * (NG - 1) + b + 1))
                if at:
                    dve.wait_ge(moments_done, at * QT)
                for i in range(QT):
                    dve.bn_stats(stat6[:, i, :], x[:, b * QT + i, :]).then_inc(stat_done, 1)
                dve.wait_ge(stat_done, (at + 1) * QT)
                for i in range(QT):
                    dve.bn_aggr(moments[b][:, i, :], stat6[:, i, :]).then_inc(moments_done, 1)

            def normalise(stage, b, i):
                tile = ln_tile(stage, b, i)
                dve.wait_ge(rstd_done, stage * NB + b + 1)
                if tile >= 2:
                    dve.wait_ge(xn_turned, tile - 1)
                dve.tensor_scalar(xn[i % 2][:, :], x[:, b * QT + i, :], moments[b][:, i, 0:1],
                                  rstd_of[b][:, i:i + 1], ALU.subtract, ALU.mult).then_inc(xn_done, 1)

            def weigh(stage, b, i):
                tile = ln_tile(stage, b, i)
                dve.wait_ge(xn_turned, tile + 1)
                if tile >= 2:
                    dve.wait_ge(n_split, tile - 1)
                dve.tensor_tensor(xw[i % 2][:, :, :], ln_bank[stage, b][i % 2][:, :].rearrange("p (k n) -> p k n", k=KT),
                                  lnw[:, :, None].to_broadcast([P, KT, P]), ALU.mult).then_inc(xn_weighted, 1)

            def n_low(stage, b, i):
                tile = ln_tile(stage, b, i)
                src = xw[i % 2][:, :, :] if stage != 1 else ln_bank[stage, b][i % 2][:, :].rearrange("p (k n) -> p k n", k=KT)
                dve.wait_ge(n_hi_done, tile + 1)
                dve.tensor_tensor(n_lo[b][:, :, i * P:(i + 1) * P], src, f(n_hi[b][:, :, i * P:(i + 1) * P]),
                                  ALU.subtract).then_inc(n_split, 1)

            def d_low(p, count):
                dve.wait_ge(d_hi_done, count)
                dve.tensor_tensor(d_lo[p][:, :], raw_d[p][:, :], f(d_hi[p][:, :]), ALU.subtract).then_inc(d_split, 1)

            def chunk(p, G, more_d):
                dve.wait_ge(silu_done, G + 1)
                if not isinstance(G, int) or G >= 2:
                    dve.wait_ge(h_split, G - 1)
                dve.tensor_tensor(hf[p][:, :], ffn_u[p][:, :], silu[p][:, :], ALU.mult).then_inc(h_done, 1)
                dve.wait_ge(h_hi_done, G + 1)
                dve.tensor_tensor(h_lo[p][:, :], hf[p][:, :], f(h_hi[p][:, :]), ALU.subtract).then_inc(h_split, 1)
                if more_d:
                    d_low(1 - p, G + 2)

            def ffn(stage, b, between):
                at = (stage * NB + b) * NC
                for c in range(2):
                    chunk(c, at + c, True)
                    between(c)
                with dve.Fori(0, (NC - 4) // 2) as k:
                    for p in range(2):
                        chunk(p, 2 * k + (at + 2 + p), True)
                between(11)
                for c in range(NC - 2, NC):
                    chunk(c % 2, at + c, b == 0 or c == NC - 2)

            def add_ffn(stage, b):
                for n, i in enumerate(Y_ORDER):
                    if n < QT - 1:
                        dve.wait_ge(ffn_y_done, (stage * NB + b) * (QT - 1) + n + 1)
                    else:
                        dve.wait_ge(down_done, (stage * NB + b + 1) * NC)
                    t = b * QT + i
                    dve.scalar_tensor_tensor(x[:, t, :], ffn_y[i][:, :], 0.5, x[:, t, :], ALU.mult,
                                             ALU.add).then_inc(ffn_y_added, 1)

            def second_half_start(stage):
                stats(stage, 1)
                normalise(stage, 1, 0)
                normalise(stage, 1, 1)
                weigh(stage, 1, 0)
                weigh(stage, 1, 1)
                n_low(stage, 1, 0)
                normalise(stage, 1, 2)
                n_low(stage, 1, 1)
                normalise(stage, 1, 3)

            def ffn_both(stage):
                second_half_start(2 * stage)

                def rest(c):
                    if c == 0:
                        weigh(2 * stage, 1, 2)
                        weigh(2 * stage, 1, 3)
                        n_low(2 * stage, 1, 2)
                        n_low(2 * stage, 1, 3)

                ffn(stage, 0, rest)
                add_ffn(stage, 0)

                def next_norm(c):
                    if stage == 0 and c == 1:
                        stats(1, 0)
                    if stage == 0 and c == 11:
                        normalise(1, 0, 0)
                        normalise(1, 0, 1)

                ffn(stage, 1, next_norm)

            def project(g, b, r):
                R = 2 * NR * g + (NR * b + r)
                src = pj_bank[(b * NR + r) % 2]
                if r < NW - 1:
                    dve.wait_ge(pj_hi_done, (2 * (NW - 1)) * g + ((NW - 1) * b + r + 1))
                if r == 0:
                    dve.tensor_tensor(k_lo[b][:, :], src[:, :], f(k_hi[b][:, :]), ALU.subtract).then_inc(pj_read, 1)
                elif r < NW - 1:
                    scale = qscales[:, ds(GH * g + (r - 1), 1)] if not isinstance(g, int) else qscales[:, GH * g + r - 1:GH * g + r]
                    dve.scalar_tensor_tensor(q_lo[b][:, r - 1, :], src[:, :], scale, f(q_hi[b][:, r - 1, :]),
                                             ALU.mult, ALU.subtract).then_inc(pj_read, 1)
                else:
                    j = 2 * (r - NW + 1)
                    V = 2 * NB * g + (2 * b + r - NW + 1)
                    halves = src[:, :].rearrange("p (j a n) -> p j a n", j=2, a=2)
                    dve.wait_ge(v_part_done, V + 1)
                    if not (isinstance(V, int) and V == 0):
                        dve.wait_ge(v_split, V)
                    dve.tensor_tensor(v_sum[:, :, :], halves[:, :, 0, :], v_part[:, :, :], ALU.add).then_inc(pj_read, 1)
                    dve.wait_ge(v_hi_done, V + 1)
                    dve.tensor_tensor(v_lo[b][:, j:j + 2, :], v_sum[:, :, :], f(v_hi[b][:, j:j + 2, :]),
                                      ALU.subtract).then_inc(v_split, 1)

            def add_out(s, i):
                b = s[1]
                Y = NB * QT * s[0] + (QT * b + QT - 1 - i)
                dve.wait_ge(y_done, Y + 1)
                dve.wait_ge(y_free, Y + 1)
                t = b * QT + i
                dve.tensor_tensor(x[:, t, :], x[:, t, :], y_bank[:, :], ALU.add).then_inc(y_free, 1)

            def fill(g, n, what):
                kind, arg = what
                b = n // 8
                if kind == "proj":
                    project(*((g, 1) if b == 0 else (g + 1, 0)), arg)
                elif kind == "out":
                    add_out((g, b), arg)
                elif kind == "stats":
                    stats(2, 0)
                elif kind == "tile":
                    if arg == 0:
                        normalise(2, 0, 0)
                        normalise(2, 0, 1)
                    weigh(2, 0, arg)
                    n_low(2, 0, arg)
                    if arg < 2:
                        normalise(2, 0, arg + 2)

            def bias_max(u, n):
                i, hp = unit(n)[1:]
                w = (i + 1) * P
                for h in range(2):
                    dve.wait_ge(s_done, 2 * u + (h + 1))
                    dve.sem_inc(scores_seen, 1)
                    head = 2 * hp + h
                    dve.tensor_tensor_reduce(scores[h][:, 0:w], s_bank[h][:, 0:w], dist[:, SEQ - w:SEQ],
                                             slope_now[:, head:head + 1], 3e38, ALU.add, ALU.min,
                                             neg_max[:, h:h + 1]).then_inc(biased, 1)

            def scale_probs(u, n):
                w = (unit(n)[1] + 1) * P
                dve.wait_ge(exp_done, 2 * u + 2)
                dve.reciprocal(row_inv[:, :], row_sum[:, :]).then_inc(inv_done, 1)
                dve.wait_ge(inv_done, u + 1)
                for h in range(2):
                    ins = dve.tensor_scalar(probs[h][:, 0:w], probs[h][:, 0:w], row_inv[:, h:h + 1], None, ALU.mult)
                ins.then_inc(p_ready, 1)

            def set_slopes(g):
                src = slopes[:, ds(GH * g, GH)] if not isinstance(g, int) else slopes[:, GH * g:GH * g + GH]
                dve.tensor_copy(slope_now[:, :], src).then_inc(slope_set, 1)
                dve.wait_ge(slope_set, g + 1)

            def slot(g, n):
                b, i, hp = unit(n)
                par = n % 2
                u = UNITS * g + n
                a_fill, b_fill = fillers(g, n)
                for m in range(n_pt(i)):
                    E = PT_BEFORE[UNITS] * g + (PT_BEFORE[n] + m + 1)
                    w = min(2, i + 1 - 2 * m) * 2 * P
                    j = slice(2 * m, 2 * m + w // (2 * P))
                    dve.wait_ge(pt_hi_done, E)
                    dve.tensor_tensor(pt_lo[par][:, j, :], pt_bank[m][:, 0:w], f(pt_hi[par][:, j, :]),
                                      ALU.subtract).then_inc(pt_split, 1)
                more = not (isinstance(g, int) and g == NG - 1 and n == UNITS - 1)
                if more:
                    if n == UNITS - 1:
                        set_slopes(g + 1)
                    bias_max(u + 1, (n + 1) % UNITS)
                for what in a_fill:
                    fill(g, n, what)
                if more:
                    scale_probs(u + 1, (n + 1) % UNITS)
                dve.wait_ge(o_hi_done, u + 1)
                o = slice(2 * hp, 2 * hp + 2)
                dve.tensor_tensor(o_lo[i % 2][:, o, :], o_bank[:, 0:2 * P], f(o_hi[i % 2][:, o, :]),
                                  ALU.subtract).then_inc(o_free, 1)
                for what in b_fill:
                    fill(g, n, what)

            dve.sem_inc(o_free, 1)
            dve.sem_inc(y_free, 1)
            dve.wait_ge(consts_in, 16 * 5)
            stats(0, 0)
            normalise(0, 0, 0)
            normalise(0, 0, 1)
            for i in range(QT):
                weigh(0, 0, i)
                n_low(0, 0, i)
                if i < 2:
                    normalise(0, 0, i + 2)
            d_low(0, 1)
            ffn_both(0)
            n_low(1, 0, 0)
            normalise(1, 0, 2)
            n_low(1, 0, 1)
            normalise(1, 0, 3)
            n_low(1, 0, 2)
            n_low(1, 0, 3)
            add_ffn(0, 1)
            project(0, 0, 0)
            stats(1, 1)
            project(0, 0, 1)
            project(0, 0, 2)
            normalise(1, 1, 0)
            normalise(1, 1, 1)
            project(0, 0, 3)
            project(0, 0, 4)
            n_low(1, 1, 0)
            normalise(1, 1, 2)
            n_low(1, 1, 1)
            normalise(1, 1, 3)
            project(0, 0, 5)
            n_low(1, 1, 2)
            n_low(1, 1, 3)
            project(0, 0, 6)
            set_slopes(0)
            bias_max(0, 0)
            scale_probs(0, 0)
            with dve.Fori(0, NG - 1) as g:
                for n in range(UNITS):
                    slot(g, n)
            for n in range(UNITS):
                slot(NG - 1, n)
            d_low(0, 2 * NC + 1)
            ffn_both(1)
            add_ffn(1, 1)

        @block.tensor
        def _(pe):
            def three(dst, w_hi, w_lo, m_hi, m_lo, first, last):
                pe.matmul(dst, w_hi, m_hi, start=first, stop=False)
                pe.matmul(dst, w_hi, m_lo, start=False, stop=False)
                return pe.matmul(dst, w_lo, m_hi, start=False, stop=last)

            def turn(stage, b, i):
                tile = ln_tile(stage, b, i)
                pe.wait_ge(xn_done, tile + 1)
                if tile >= 2:
                    pe.wait_ge(n_split, tile - 1)
                dst = ln_bank[stage, b][i % 2]
                for k in range(KT):
                    ins = pe.transpose(dst[:, k * P:(k + 1) * P], xn[i % 2][:, k * P:(k + 1) * P], ident[:, :])
                ins.then_inc(xn_turned, 1)

            def gate_up(b, p, G):
                pe.wait_ge(gu_split, G + 1)
                if not isinstance(G, int) or G >= 2:
                    pe.wait_ge(h_done, G - 1)
                for m, dst in enumerate((ffn_g[p], ffn_u[p])):
                    for k in range(KT):
                        ins = three(dst[:, :], gu_hi[p][:, m, k, :], gu_lo[p][:, m, k, :],
                                    n_hi[b][:, k, :], n_lo[b][:, k, :], k == 0, k == KT - 1)
                ins.then_inc(gu_done, 1)

            def down(p, G, first, last):
                pe.wait_ge(h_split, G + 1)
                pe.wait_ge(d_split, G + 1)
                for i in Y_ORDER:
                    tile = slice(i * P, (i + 1) * P)
                    ins = three(ffn_y[i][:, :], h_hi[p][:, tile], h_lo[p][:, tile], d_hi[p][:, :], d_lo[p][:, :],
                                first, last)
                    if last and i != Y_ORDER[-1]:
                        ins.then_inc(ffn_y_done, 1)
                ins.then_inc(down_done, 1)

            def ffn_both(stage):
                at = stage * NB * NC
                if stage:
                    pe.wait_ge(y_free, 1 + NG * NB * QT)
                pe.wait_ge(n_split, (2 * stage * NB + 1) * QT)
                gate_up(0, 0, at)
                turn(2 * stage, 1, 0)
                turn(2 * stage, 1, 1)
                for b in range(NB):
                    first = at + b * NC
                    gate_up(b, 1, first + 1)
                    if b == 0:
                        turn(2 * stage, 1, 2)
                        turn(2 * stage, 1, 3)
                        pe.wait_ge(n_split, (2 * stage * NB + 2) * QT)
                    if stage or b:
                        pe.wait_ge(ffn_y_added, (stage * NB + b) * QT)
                    down(0, first, True, False)
                    gate_up(b, 0, first + 2)
                    down(1, first + 1, False, False)
                    with pe.Fori(0, (NC - 4) // 2) as k:
                        for p in range(2):
                            gate_up(b, 1 - p, 2 * k + (first + 3 + p))
                            down(p, 2 * k + (first + 2 + p), False, False)
                    gate_up(b, 1, first + NC - 1)
                    down(0, first + NC - 2, False, False)
                    if b == 0:
                        gate_up(1, 0, first + NC)
                    elif stage == 0:
                        turn(1, 0, 0)
                        turn(1, 0, 1)
                    down(1, first + NC - 1, False, True)

            def project(g, b, r):
                R = 2 * NR * g + (NR * b + r)
                dst = pj_bank[(b * NR + r) % 2]
                pe.wait_ge(wq_split, 10 * g + (min(r, NW - 1) + 1))
                if not isinstance(R, int) or R >= 2:
                    pe.wait_ge(pj_read, R - 1)
                if r < NW - 1:
                    for k in range(KT):
                        ins = three(dst[:, :], wq_hi[r][:, k, :], wq_lo[r][:, k, :], n_hi[b][:, k, :],
                                    n_lo[b][:, k, :], k == 0, k == KT - 1)
                else:
                    for j in range(2):
                        tile = slice((2 * (r - NW + 1) + j) * P, (2 * (r - NW + 1) + j + 1) * P)
                        for k in range(KT):
                            both = wv[:, k, :, :]
                            out_ = dst[:, 2 * P * j:2 * P * (j + 1)]
                            pe.matmul(out_, n_hi[b][:, k, tile], both, start=k == 0, stop=False)
                            ins = pe.matmul(out_, n_lo[b][:, k, tile], both, start=False, stop=k == KT - 1)
                ins.then_inc(pj_done, 1)

            def score(g, n, u):
                b, i, hp = unit(n)
                w = max((i + 1) * P, 2 * P)
                if n % 8 < 2:
                    pe.wait_ge(pj_read, 2 * NR * g + (NR * b + (3 if n % 8 == 0 else 5)))
                for h in range(2):
                    q = (slice(None), 2 * hp + h, slice(i * P, (i + 1) * P))
                    three(s_bank[h][:, 0:w], q_hi[b][q], q_lo[b][q], k_hi[b][:, 0:w], k_lo[b][:, 0:w],
                          True, True).then_inc(s_done, 1)

            def out_tile(g, b, i):
                Y = NB * QT * g + (QT * b + QT - 1 - i)
                pe.wait_ge(o_free, UNITS * g + (8 * b + 2 * (QT - 1 - i) + 3))
                pe.wait_ge(y_free, Y + 1)
                for h in range(GH):
                    if b == 0 and i == QT - 1:
                        pe.wait_ge(wq_split, 10 * g + (NW + h + 1))
                    ins = three(y_bank[:, :], o_hi[i % 2][:, h, :], o_lo[i % 2][:, h, :], wo_hi[h][:, :],
                                wo_lo[h][:, :], h == 0, h == GH - 1)
                ins.then_inc(y_done, 1)

            def fill(g, n, what):
                kind, arg = what
                b = n // 8
                if kind == "proj":
                    project(*((g, 1) if b == 0 else (g + 1, 0)), arg)
                elif kind == "out":
                    out_tile(g, b, arg)
                elif kind == "tile":
                    turn(2, 0, arg)

            def slot(g, n):
                b, i, hp = unit(n)
                par = n % 2
                u = UNITS * g + n
                a_fill, b_fill = fillers(g, n)
                pe.wait_ge(p_ready, u + 1)
                for m in range(n_pt(i)):
                    for j in range(2 * m, min(2 * m + 2, i + 1)):
                        for h in range(2):
                            at = (j % 2 * 2 + h) * P
                            ins = pe.transpose(pt_bank[m][:, at:at + P], probs[h][:, j * P:(j + 1) * P], ident[:, :])
                    ins.then_inc(pt_done, 1)
                if not (isinstance(g, int) and g == NG - 1 and n == UNITS - 1):
                    nxt = (n + 1) % UNITS
                    score(g if nxt else g + 1, nxt, u + 1)
                for what in a_fill:
                    fill(g, n, what)
                if n % 8 == 0:
                    pe.wait_ge(v_split, 2 * NB * g + (2 * b + 2))
                pe.wait_ge(o_free, u + 1)
                for j in range(i + 1):
                    if j % 2 == 0:
                        pe.wait_ge(pt_split, PT_BEFORE[UNITS] * g + (PT_BEFORE[n] + j // 2 + 1))
                    ins = three(o_bank[:, 0:2 * P], v_hi[b][:, j, :], v_lo[b][:, j, :], pt_hi[par][:, j, :],
                                pt_lo[par][:, j, :], j == 0, j == i)
                ins.then_inc(pv_done, 1)
                for what in b_fill:
                    fill(g, n, what)

            pe.wait_ge(consts_in, 16 * 5)
            for i in range(QT):
                turn(0, 0, i)
            ffn_both(0)
            turn(1, 0, 2)
            turn(1, 0, 3)
            pe.wait_ge(n_split, 3 * QT)
            for r in range(4):
                project(0, 0, r)
            turn(1, 1, 0)
            turn(1, 1, 1)
            project(0, 0, 4)
            turn(1, 1, 2)
            turn(1, 1, 3)
            project(0, 0, 5)
            project(0, 0, 6)
            pe.wait_ge(n_split, 4 * QT)
            score(0, 0, 0)
            with pe.Fori(0, NG - 1) as g:
                for n in range(UNITS):
                    slot(g, n)
            for n in range(UNITS):
                slot(NG - 1, n)
            ffn_both(1)


_INS = ["x", "w_gu", "w_d", "ln_w", "w_qkv", "w_o", "ident", "dist", "slopes", "qscales"]


def kernel(L0_attn_hidden_states, L0_attn_w_qkv, L0_attn_w_o, L0_ffn_ln_w, L0_ffn_gate_w, L0_ffn_up_w, L0_ffn_down_w):
    import numpy as np
    import concourse.bacc as bacc
    from concourse.bass_utils import run_bass_kernel_spmd

    x = np.asarray(L0_attn_hidden_states)
    gate, up, down = (np.asarray(w) for w in (L0_ffn_gate_w, L0_ffn_up_w, L0_ffn_down_w))
    cols = [w.reshape(NC, P, KT, P).transpose(0, 3, 2, 1).reshape(NC, P, KT * P) for w in (gate, up)]
    w_gu = np.ascontiguousarray(np.concatenate(cols, axis=2))
    w_d = np.ascontiguousarray(down.T.reshape(NC, P, D))
    ln_w = np.ascontiguousarray(np.asarray(L0_ffn_ln_w).reshape(KT, P).T)
    wqkv = np.asarray(L0_attn_w_qkv).reshape(KT, P, NG * (GH + 2), P).transpose(2, 1, 0, 3).reshape(-1, P, D)
    nq = NG * GH
    order = [c for g in range(NG) for c in [nq + g] + [GH * g + h for h in range(GH)] + [nq + NG + g]]
    w_qkv = np.ascontiguousarray(wqkv[order])
    w_o = np.ascontiguousarray(np.asarray(L0_attn_w_o).reshape(NG * GH, P, D))
    ident = np.eye(P, dtype=np.float32)
    rel = np.arange(P)[:, None] + (SEQ - P) - np.arange(SEQ)[None, :]
    dist = np.where(rel >= 0, np.sqrt(np.maximum(rel, 0)), MASKED).astype(np.float32)
    slope = (2.0 ** (-8.0 / nq)) ** np.arange(1, nq + 1)
    slopes = np.ascontiguousarray(np.broadcast_to(slope.astype(np.float32), (P, nq)))
    qscales = np.ascontiguousarray(np.broadcast_to((-SCALE / slope).astype(np.float32), (P, nq)))
    arrays = dict(zip(_INS, (x.reshape(-1, D), w_gu, w_d, ln_w, w_qkv, w_o, ident, dist, slopes, qscales)))

    nc = bacc.Bacc("TRN2", target_bir_lowering=False, num_devices=1)
    args = [nc.dram_tensor(f"{n}_dram", arrays[n].shape, F32, kind="ExternalInput").ap() for n in _INS]
    args.append(nc.dram_tensor("out_dram", [NB * SEQ, D], F32, kind="ExternalOutput").ap())
    macaron_kernel(nc, *args)
    r = run_bass_kernel_spmd(nc, [{f"{n}_dram": arrays[n] for n in _INS}], core_ids=[0])
    return r.results[0]["out_dram"].reshape(x.shape)
```

```python
from contextlib import ExitStack

import concourse.bass as bass
from concourse import mybir

F32 = mybir.dt.float32
F32R = mybir.dt.float32r
ALU = mybir.AluOpType
ACT = mybir.ActivationFunctionType

P = 128
D = 512
KT = D // P
SEQ = 512
NB = 2
QT = SEQ // P
INNER = 1792
NC = INNER // P
NG = 8
GH = 4
EPS = 1e-5
SCALE = float(P) ** -0.5
MASKED = 1e37

NW = 6
NR = 7
Y_ORDER = (2, 3, 0, 1)
RAWQ = 5
UNITS = 16
ds = bass.ds


def macaron_kernel(nc, x_in, w_gu, w_d, ln_w, w_qkv, w_o, ident_in, dist_in, slope_in, qscale_in, out):
    ctx = ExitStack()
    with ctx:
        def sem(name):
            return ctx.enter_context(nc.semaphore(name))

        base = (nc.sbuf_base + 31) // 32 * 32
        arena_bytes = (nc.sbuf_bytes_remaining - 64) // 32 * 32
        ctx.enter_context(nc.sbuf_tensor("arena", [P, arena_bytes], mybir.dt.uint8))
        cursor = [base]

        def place(name, shape, dt, at=None):
            size = 4
            for n in shape[1:]:
                size *= n
            where = cursor[0] if at is None else at
            if at is None:
                cursor[0] += (size + 31) // 32 * 32
                assert cursor[0] <= base + arena_bytes, (name, cursor[0] - base, arena_bytes)
            return nc.alloc_sbuf_tensor_at(name, shape, dt, offset=where)

        x = place("x", [P, NB * QT, D], F32)
        n_hi = [place(f"n_hi{b}", [P, KT, SEQ], F32R) for b in range(NB)]
        n_lo = [place(f"n_lo{b}", [P, KT, SEQ], F32R) for b in range(NB)]
        ident = place("ident", [P, P], F32)
        dist = place("dist", [P, SEQ], F32)
        slopes = place("slopes", [P, NG * GH], F32)
        qscales = place("qscales", [P, NG * GH], F32)
        slope_now = place("slope_now", [P, GH], F32)
        lnw = place("lnw", [P, KT], F32)
        stat6 = place("stat6", [P, QT, 6], F32)
        moments = [place(f"moments{b}", [P, QT, 2], F32) for b in range(NB)]
        half_power = place("half_power", [P, QT], F32)
        spread = place("spread", [P, QT], F32)
        rstd_of = [place(f"rstd_of{b}", [P, QT], F32) for b in range(NB)]
        neg_max = place("neg_max", [P, 2], F32)
        row_sum = place("row_sum", [P, 2], F32)
        row_inv = place("row_inv", [P, 2], F32)
        xn = [place(f"xn{n}", [P, D], F32) for n in range(2)]
        xw = [place(f"xw{n}", [P, KT, P], F32) for n in range(2)]
        raw_gu = [place(f"raw_gu{p}", [P, 2 * KT * P], F32) for p in range(2)]
        raw_d = [place(f"raw_d{p}", [P, D], F32) for p in range(2)]
        raw_q = [place(f"raw_q{p}", [P, D], F32) for p in range(RAWQ)]
        wo_hi = [place(f"wo_hi{h}", [P, D], F32R) for h in range(GH)]
        wo_lo = [place(f"wo_lo{h}", [P, D], F32R) for h in range(GH)]

        w_at = cursor[0]
        gu_hi = [place(f"gu_hi{p}", [P, 2, KT, P], F32R) for p in range(2)]
        gu_lo = [place(f"gu_lo{p}", [P, 2, KT, P], F32R) for p in range(2)]
        d_hi = [place(f"d_hi{p}", [P, D], F32R) for p in range(2)]
        d_lo = [place(f"d_lo{p}", [P, D], F32R) for p in range(2)]
        chunk = 4 * KT * P
        wq_hi = [place(f"wq_hi{r}", [P, KT, P], F32R, w_at + 2 * r * chunk) for r in range(5)]
        wq_lo = [place(f"wq_lo{r}", [P, KT, P], F32R, w_at + (2 * r + 1) * chunk) for r in range(5)]
        wv = place("wv", [P, KT, 2, P], F32R, w_at + 10 * chunk)

        h_at = cursor[0]
        pt_hi = [place(f"pt_hi{p}", [P, QT, 2 * P], F32R) for p in range(2)]
        pt_lo = [place(f"pt_lo{p}", [P, QT, 2 * P], F32R) for p in range(2)]
        row = 4 * SEQ
        silu = [place(f"silu{p}", [P, SEQ], F32, h_at + p * row) for p in range(2)]
        hf = [place(f"hf{p}", [P, SEQ], F32, h_at + (2 + p) * row) for p in range(2)]
        h_hi = [place(f"h_hi{p}", [P, SEQ], F32R, h_at + (4 + p) * row) for p in range(2)]
        h_lo = [place(f"h_lo{p}", [P, SEQ], F32R, h_at + (6 + p) * row) for p in range(2)]

        q_hi = [place(f"q_hi{b}", [P, GH, SEQ], F32R) for b in range(NB)]
        q_lo = [place(f"q_lo{b}", [P, GH, SEQ], F32R) for b in range(NB)]
        k_hi = [place(f"k_hi{b}", [P, SEQ], F32R) for b in range(NB)]
        k_lo = [place(f"k_lo{b}", [P, SEQ], F32R) for b in range(NB)]
        v_hi = [place(f"v_hi{b}", [P, QT, P], F32R) for b in range(NB)]
        v_lo = [place(f"v_lo{b}", [P, QT, P], F32R) for b in range(NB)]
        v_part = place("v_part", [P, 2, P], F32)
        v_sum = place("v_sum", [P, 2, P], F32)
        scores = [place(f"scores{h}", [P, SEQ], F32) for h in range(2)]
        probs = [[place(f"probs{p}{h}", [P, SEQ], F32) for h in range(2)] for p in range(2)]
        o_hi = [place(f"o_hi{p}", [P, GH, P], F32R) for p in range(2)]
        o_lo = [place(f"o_lo{p}", [P, GH, P], F32R) for p in range(2)]

        bank = [ctx.enter_context(nc.psum_tensor(f"bank{n}", [P, 512], F32)) for n in range(8)]
        ffn_y = bank[0:4]
        ffn_g, ffn_u = [bank[4], bank[5]], [bank[6], bank[7]]
        s_bank, pt_bank, o_bank, y_bank = bank[0:2], bank[2:4], bank[5], bank[7]
        pj_bank = [bank[4], bank[6]]
        ln_bank = {(0, 0): bank[0:2], (0, 1): ffn_u, (1, 0): [bank[4], bank[6]],
                   (1, 1): [bank[5], bank[7]], (2, 0): pj_bank, (2, 1): ffn_u}

        consts_in = sem("consts_in")
        x_in_sem = [sem(f"x_in{i}") for i in range(QT + 1)]
        gu_in = [sem(f"gu_in{p}") for p in range(2)]
        d_in = [sem(f"d_in{p}") for p in range(2)]
        q_in = [sem(f"q_in{p}") for p in range(RAWQ)]
        out_written = sem("out_written")
        stat_done, moments_done, power_set, spread_done, rstd_done = (sem(n) for n in ("stat_done", "moments_done", "power_set", "spread_done", "rstd_done"))
        xn_done, xn_turned, xn_weighted, n_hi_done, n_split = (sem(n) for n in ("xn_done", "xn_turned", "xn_weighted", "n_hi_done", "n_split"))
        gu_hi_done, gu_split, d_hi_done, d_split = (sem(n) for n in ("gu_hi_done", "gu_split", "d_hi_done", "d_split"))
        gu_done, silu_done, h_done, h_hi_done, h_split = (sem(n) for n in ("gu_done", "silu_done", "h_done", "h_hi_done", "h_split"))
        down_done, ffn_y_done, ffn_y_added = (sem(n) for n in ("down_done", "ffn_y_done", "ffn_y_added"))
        wq_hi_done, wq_split = (sem(n) for n in ("wq_hi_done", "wq_split"))
        pj_done, pj_hi_done, pj_read = (sem(n) for n in ("pj_done", "pj_hi_done", "pj_read"))
        v_part_done, v_hi_done, v_split = (sem(n) for n in ("v_part_done", "v_hi_done", "v_split"))
        slope_set, s_done, biased, exp_done, inv_done, p_ready = (sem(n) for n in ("slope_set", "s_done", "biased", "exp_done", "inv_done", "p_ready"))
        pt_done, pt_hi_done, pt_split = (sem(n) for n in ("pt_done", "pt_hi_done", "pt_split"))
        pv_done, o_hi_done, o_free = (sem(n) for n in ("pv_done", "o_hi_done", "o_free"))
        scores_seen, chunk_begun = (sem(n) for n in ("scores_seen", "chunk_begun"))
        y_done, y_free = (sem(n) for n in ("y_done", "y_free"))

        f = lambda t: t.bitcast(F32)

        def ln_tile(stage, b, i):
            return (stage * NB + b) * QT + i

        def unit(n):
            return n // 8, QT - 1 - n % 8 // 2, n % 2

        def n_pt(i):
            return (i + 2) // 2

        PT_BEFORE = [sum(n_pt(unit(m)[1]) for m in range(n)) for n in range(UNITS + 1)]
        FILL = {0: (["proj 0", "out 0"], []), 1: (["proj 1"], []), 2: (["proj 2"], ["out 3"]),
                3: (["proj 3"], []), 4: (["proj 4"], ["out 2"]), 5: (["proj 5"], []),
                6: (["proj 6"], []), 7: (["out 1"], [])}
        LAST_FILL = {0: (["out 0", "stats 0"], []), 1: (["norm 0"], []), 2: (["turn 0"], ["out 3"]),
                     3: (["turn 1"], []), 4: (["turn 2"], ["out 2"]), 5: (["turn 3"], []),
                     6: (["gate 0"], []), 7: (["out 1"], ["up 0"])}

        def ahead(g, n, by):
            if n + by < UNITS:
                return g, n + by
            return None if isinstance(g, int) and g == NG - 1 else (g + 1, n + by - UNITS)

        def fillers(g, n):
            last = isinstance(g, int) and g == NG - 1 and n >= 8
            b = n // 8

            def full(what):
                kind, arg = what.split()
                if kind == "proj":
                    return (kind, g, 1, int(arg)) if b == 0 else (kind, g + 1, 0, int(arg))
                if what == "out 0":
                    if b == 0 and isinstance(g, int) and g == 0:
                        return ("none", 0, 0, 0)
                    return (kind, g, 0, 0) if b else (kind, g - 1, 1, 0)
                return kind, g, b, int(arg)

            a, b_ = (LAST_FILL if last else FILL)[n % 8]
            return [full(w) for w in a], [full(w) for w in b_]

        block = ctx.enter_context(nc.Block())

        @block.sync
        def _(sp):
            x_rows = x_in.rearrange("(t p) d -> p t d", p=P)
            out_rows = out.rearrange("(t p) d -> p t d", p=P)

            def load_gu(c, parity, before):
                sp.wait_ge(gu_split, before)
                sp.dma_start(raw_gu[parity][:, :], w_gu[c]).then_inc(gu_in[parity], 16)

            def load_d(c, parity, before):
                sp.wait_ge(d_split, before)
                sp.dma_start(raw_d[parity][:, :], w_d[c]).then_inc(d_in[parity], 16)

            def load_ffn_first(stage):
                for c in range(2):
                    if stage == 0:
                        sp.dma_start(raw_gu[c][:, :], w_gu[c]).then_inc(gu_in[c], 16)
                        sp.dma_start(raw_d[c][:, :], w_d[c]).then_inc(d_in[c], 16)
                    else:
                        load_gu(c, c, 2 * NC * stage - 1 + c)
                        load_d(c, c, 2 * NC * stage - 1 + c)

            def load_ffn_rest(stage):
                for h in range(NB):
                    first = 2 if h == 0 else 0
                    at = (stage * NB + h) * NC
                    with sp.Fori(0, (NC - first) // 2) as k:
                        for p in range(2):
                            c = 2 * k + (first + p)
                            for load, src, dst, done, s in ((load_gu, w_gu, raw_gu, gu_split, gu_in),
                                                            (load_d, w_d, raw_d, d_split, d_in)):
                                sp.wait_ge(done, c + (at - 1))
                                sp.dma_start(dst[p][:, :], src[ds(c, 1)].rearrange("a p n -> (a p) n")).then_inc(s[p], 16)

            def load_group(g):
                for q in range(NW + GH):
                    if isinstance(g, int):
                        if 10 * g + q >= RAWQ:
                            sp.wait_ge(wq_split, 10 * g + q - RAWQ + 1)
                        src = w_qkv[NW * g + q] if q < NW else w_o[GH * g + q - NW]
                    else:
                        sp.wait_ge(wq_split, 10 * g + (q - RAWQ + 1))
                        src = w_qkv[ds(NW * g + q, 1)] if q < NW else w_o[ds(GH * g + (q - NW), 1)]
                        src = src.rearrange("a p n -> (a p) n")
                    sp.dma_start(raw_q[q % RAWQ][:, :], src).then_inc(q_in[q % RAWQ], 16)

            for i in range(QT):
                sp.dma_start(x[:, i, :], x_rows[:, i, :]).then_inc(x_in_sem[i], 16)
            load_ffn_first(0)
            sp.dma_start(x[:, QT:, :], x_rows[:, QT:, :]).then_inc(x_in_sem[QT], 16)
            load_ffn_rest(0)
            load_group(0)
            with sp.Fori(1, NG) as g:
                load_group(g)
            load_ffn_first(1)
            load_ffn_rest(1)
            for b in range(NB):
                for n, i in enumerate(Y_ORDER):
                    sp.wait_ge(ffn_y_added, (NB + b) * QT + n + 1)
                    t = b * QT + i
                    sp.dma_start(out_rows[:, t, :], x[:, t, :]).then_inc(out_written, 16)
            sp.wait_ge(out_written, 16 * NB * QT)

        @block.gpsimd
        def _(pool):
            def rstd(stage, b):
                pool.wait_ge(moments_done, (stage * NB + b + 1) * QT)
                mul, add = (1.0, EPS) if stage == 1 else (1.0 + EPS, EPS * EPS)
                pool.tensor_scalar(spread[:, :], moments[b][:, :, 1], mul, add, ALU.mult, ALU.add).then_inc(spread_done, 1)
                pool.wait_ge(spread_done, stage * NB + b + 1)
                pool.tensor_tensor(rstd_of[b][:, :], spread[:, :], half_power[:, :], ALU.pow).then_inc(rstd_done, 1)

            def gu_low(p, count):
                pool.wait_ge(gu_hi_done, count)
                pool.tensor_tensor(gu_lo[p][:, :, :, :], raw_gu[p][:, :], f(gu_hi[p][:, :, :, :]),
                                   ALU.subtract).then_inc(gu_split, 1)

            def ffn(stage):
                at = stage * NB * NC
                with pool.Fori(0, (2 * NC - 4) // 2) as k:
                    for p in range(2):
                        gu_low(p, 2 * k + (at + 2 + p + 1))
                if stage == 0:
                    rstd(1, 0)
                for p in range(2):
                    gu_low(p, at + 2 * NC - 2 + p + 1)

            def split_group(g, prev):
                for q in range(NW + GH):
                    load_no = 2 * g + (q // RAWQ + 1)
                    pool.wait_ge(q_in[q % RAWQ], 16 * load_no)
                    if prev is None:
                        if q == 0:
                            pool.wait_ge(gu_done, 2 * NC)
                        if q == 4:
                            pool.wait_ge(down_done, 2 * NC)
                    else:
                        done, count = ((pj_done, 2 * NR * prev + (NR + q + 1)) if q < NW - 1 else
                                       (pj_done, 2 * NR * prev + 2 * NR) if q == NW - 1 else
                                       (y_done, 2 * QT * prev + 2 * QT))
                        pool.wait_ge(done, count)
                        pool.sem_inc(chunk_begun, 1)
                    raw = raw_q[q % RAWQ]
                    if q < NW - 1:
                        hi, lo, src = wq_hi[q][:, :, :], wq_lo[q][:, :, :], raw[:, :].rearrange("p (k n) -> p k n", k=KT)
                    elif q == NW - 1:
                        hi, lo, src = wv[:, :, 0, :], wv[:, :, 1, :], raw[:, :].rearrange("p (k n) -> p k n", k=KT)
                    else:
                        hi, lo, src = wo_hi[q - NW][:, :], wo_lo[q - NW][:, :], raw[:, :]
                    pool.tensor_scalar(hi, src, 1.0, 0.0, ALU.mult, ALU.add).then_inc(wq_hi_done, 1)
                    pool.wait_ge(wq_hi_done, 10 * g + (q + 1))
                    pool.tensor_tensor(lo, src, f(hi), ALU.subtract).then_inc(wq_split, 1)
                    if prev is None and q == 3:
                        rstd(1, 1)

            pool.memset(half_power[:, :], -0.5).then_inc(power_set, 1)
            pool.wait_ge(power_set, 1)
            rstd(0, 0)
            gu_low(0, 1)
            gu_low(1, 2)
            rstd(0, 1)
            ffn(0)
            split_group(0, None)
            with pool.Fori(0, NG - 1) as g:
                split_group(g + 1, g)
            rstd(2, 0)
            gu_low(0, 2 * NC + 1)
            gu_low(1, 2 * NC + 2)
            rstd(2, 1)
            ffn(1)

        @block.scalar
        def _(act):
            def n_high(stage, b, i):
                tile = ln_tile(stage, b, i)
                if stage == 1:
                    act.wait_ge(xn_turned, tile + 1)
                    src = ln_bank[stage, b][i % 2][:, :].rearrange("p (k n) -> p k n", k=KT)
                else:
                    act.wait_ge(xn_weighted, (stage // 2 * NB + b) * QT + i + 1)
                    src = xw[i % 2][:, :, :]
                act.copy(n_hi[b][:, :, i * P:(i + 1) * P], src).then_inc(n_hi_done, 1)

            def gu_high(p, landed, count):
                act.wait_ge(gu_in[p], landed)
                if not isinstance(count, int) or count >= 2:
                    act.wait_ge(gu_done, count - 1)
                act.copy(gu_hi[p][:, :, :, :], raw_gu[p][:, :]).then_inc(gu_hi_done, 1)

            def d_high(p, landed, count):
                act.wait_ge(d_in[p], landed)
                if not isinstance(count, int) or count >= 2:
                    act.wait_ge(down_done, count - 1)
                act.copy(d_hi[p][:, :], raw_d[p][:, :]).then_inc(d_hi_done, 1)

            def chunk(p, G, half_G, more_gu, more_d):
                act.wait_ge(gu_done, G + 1)
                act.activation(silu[p][:, :], ffn_g[p][:, :], ACT.Silu).then_inc(silu_done, 1)
                if more_gu:
                    gu_high(p, 16 * (half_G + 2), G + 2)
                act.wait_ge(h_done, G + 1)
                if not isinstance(G, int) or G >= 2:
                    act.wait_ge(down_done, G - 1)
                act.copy(h_hi[p][:, :], hf[p][:, :]).then_inc(h_hi_done, 1)
                if more_d:
                    d_high(1 - p, 16 * (half_G + p + 1), G + 1)

            def ffn(stage, b):
                at = (stage * NB + b) * NC
                for c in range(4):
                    chunk(c % 2, at + c, (at + c) // 2, True, True)
                    if b == 0 and c:
                        n_high(2 * stage, 1, c - 1)
                with act.Fori(0, (NC - 6) // 2) as k:
                    for p in range(2):
                        chunk(p, 2 * k + (at + 4 + p), k + (at // 2 + 2), True, True)
                for c in range(NC - 2, NC):
                    chunk(c % 2, at + c, (at + c) // 2, b == 0, b == 0 or c == NC - 2)
                    if b == 0 and c == NC - 2:
                        n_high(2 * stage, 1, 3)

            def project(g, b, r):
                R = 2 * NR * g + (NR * b + r)
                src = pj_bank[(b * NR + r) % 2]
                act.wait_ge(pj_done, R + 1)
                if r == 0:
                    act.copy(k_hi[b][:, :], src[:, :]).then_inc(pj_hi_done, 1)
                elif r < NW - 1:
                    scale = qscales[:, ds(GH * g + (r - 1), 1)] if not isinstance(g, int) else qscales[:, GH * g + r - 1:GH * g + r]
                    act.activation(q_hi[b][:, r - 1, :], src[:, :], ACT.Copy, scale=scale).then_inc(pj_hi_done, 1)
                else:
                    j = 2 * (r - NW + 1)
                    V = 2 * NB * g + (2 * b + r - NW + 1)
                    halves = src[:, :].rearrange("p (j a n) -> p j a n", j=2, a=2)
                    act.copy(v_part[:, :, :], halves[:, :, 1, :]).then_inc(v_part_done, 1)
                    act.wait_ge(pj_read, R + 1)
                    act.copy(v_hi[b][:, j:j + 2, :], v_sum[:, :, :]).then_inc(v_hi_done, 1)

            def fill(kind, g, b, arg):
                if kind == "proj":
                    project(g, b, arg)
                elif kind == "stats":
                    act.wait_ge(pj_done, NG * NB * NR)
                    gu_high(0, 16 * (NC + 1), NB * NC)
                elif kind == "norm":
                    gu_high(1, 16 * (NC + 1), NB * NC + 1)
                    d_high(0, 16 * (NC + 1), NB * NC)
                elif kind == "turn":
                    n_high(2, 0, arg)

            def exps(g, n):
                w = (unit(n)[1] + 1) * P
                for h in range(2):
                    act.wait_ge(biased, 2 * UNITS * g + (2 * n + h + 1))
                    act.activation(probs[n % 2][h][:, 0:w], scores[h][:, 0:w], ACT.Exp, bias=neg_max[:, h:h + 1],
                                   scale=-1.0, accum_out=row_sum[:, h:h + 1]).then_inc(exp_done, 1)

            def slot(g, n):
                b, i, hp = unit(n)
                par = n % 2
                u = UNITS * g + n
                a_fill, b_fill = fillers(g, n)
                for m in range(n_pt(i)):
                    E = PT_BEFORE[UNITS] * g + (PT_BEFORE[n] + m + 1)
                    w = min(2, i + 1 - 2 * m) * 2 * P
                    act.wait_ge(pt_done, E)
                    act.copy(pt_hi[par][:, 2 * m:2 * m + w // (2 * P), :],
                             pt_bank[m][:, 0:w]).then_inc(pt_hi_done, 1)
                if ahead(g, n, 2):
                    exps(*ahead(g, n, 2))
                for what in a_fill:
                    fill(*what)
                act.wait_ge(pv_done, u + 1)
                act.copy(o_hi[i % 2][:, 2 * hp:2 * hp + 2, :], o_bank[:, 0:2 * P]).then_inc(o_hi_done, 1)
                for what in b_fill:
                    fill(*what)

            for dst, src in ((ident, ident_in), (lnw, ln_w), (dist, dist_in), (slopes, slope_in), (qscales, qscale_in)):
                act.dma_start(dst[:, :], src).then_inc(consts_in, 16)
            act.wait_ge(consts_in, 16 * 5)
            gu_high(0, 16, 0)
            d_high(0, 16, 0)
            gu_high(1, 16, 1)
            for i in range(QT):
                n_high(0, 0, i)
            ffn(0, 0)
            ffn(0, 1)
            for i in range(QT):
                n_high(1, 0, i)
            for r in range(5):
                project(0, 0, r)
            n_high(1, 1, 0)
            n_high(1, 1, 1)
            project(0, 0, 5)
            n_high(1, 1, 2)
            n_high(1, 1, 3)
            project(0, 0, 6)
            exps(0, 0)
            exps(0, 1)
            slot(0, 0)
            with act.Fori(0, NG - 1) as g:
                for n in range(1, UNITS):
                    slot(g, n)
                slot(g + 1, 0)
            for n in range(1, UNITS):
                slot(NG - 1, n)
            ffn(1, 0)
            ffn(1, 1)

        @block.vector
        def _(dve):
            def stats(stage, b):
                at = stage * NB + b
                if stage == 0:
                    dve.wait_ge(x_in_sem[b * QT], 16)
                elif stage == 1:
                    dve.wait_ge(ffn_y_added, (b + 1) * QT)
                else:
                    dve.wait_ge(y_free, 1 + QT * (NB * (NG - 1) + b + 1))
                if at:
                    dve.wait_ge(moments_done, at * QT)
                for i in range(QT):
                    if stage == 0 and b == 0:
                        dve.wait_ge(x_in_sem[i], 16)
                    dve.bn_stats(stat6[:, i, :], x[:, b * QT + i, :]).then_inc(stat_done, 1)
                dve.wait_ge(stat_done, (at + 1) * QT)
                for i in range(QT):
                    dve.bn_aggr(moments[b][:, i, :], stat6[:, i, :]).then_inc(moments_done, 1)

            def normalise(stage, b, i):
                tile = ln_tile(stage, b, i)
                dve.wait_ge(rstd_done, stage * NB + b + 1)
                if tile >= 2:
                    dve.wait_ge(xn_turned, tile - 1)
                dve.tensor_scalar(xn[i % 2][:, :], x[:, b * QT + i, :], moments[b][:, i, 0:1],
                                  rstd_of[b][:, i:i + 1], ALU.subtract, ALU.mult).then_inc(xn_done, 1)

            def weigh(stage, b, i):
                tile = ln_tile(stage, b, i)
                dve.wait_ge(xn_turned, tile + 1)
                if tile >= 2:
                    dve.wait_ge(n_split, tile - 1)
                dve.tensor_tensor(xw[i % 2][:, :, :], ln_bank[stage, b][i % 2][:, :].rearrange("p (k n) -> p k n", k=KT),
                                  lnw[:, :, None].to_broadcast([P, KT, P]), ALU.mult).then_inc(xn_weighted, 1)

            def n_low(stage, b, i):
                tile = ln_tile(stage, b, i)
                src = xw[i % 2][:, :, :] if stage != 1 else ln_bank[stage, b][i % 2][:, :].rearrange("p (k n) -> p k n", k=KT)
                dve.wait_ge(n_hi_done, tile + 1)
                dve.tensor_tensor(n_lo[b][:, :, i * P:(i + 1) * P], src, f(n_hi[b][:, :, i * P:(i + 1) * P]),
                                  ALU.subtract).then_inc(n_split, 1)

            def d_low(p, count):
                dve.wait_ge(d_hi_done, count)
                dve.tensor_tensor(d_lo[p][:, :], raw_d[p][:, :], f(d_hi[p][:, :]), ALU.subtract).then_inc(d_split, 1)

            def chunk(p, G, more_d):
                dve.wait_ge(silu_done, G + 1)
                if not isinstance(G, int) or G >= 2:
                    dve.wait_ge(h_split, G - 1)
                dve.tensor_tensor(hf[p][:, :], ffn_u[p][:, :], silu[p][:, :], ALU.mult).then_inc(h_done, 1)
                dve.wait_ge(h_hi_done, G + 1)
                dve.tensor_tensor(h_lo[p][:, :], hf[p][:, :], f(h_hi[p][:, :]), ALU.subtract).then_inc(h_split, 1)
                if more_d:
                    d_low(1 - p, G + 2)

            def second_tile(stage, i):
                weigh(stage, 1, i)
                n_low(stage, 1, i)
                if i < 2:
                    normalise(stage, 1, i + 2)

            def ffn(stage, b):
                at = (stage * NB + b) * NC
                for c in range(4):
                    chunk(c % 2, at + c, True)
                    if b == 0 and c == 0:
                        normalise(2 * stage, 1, 0)
                        normalise(2 * stage, 1, 1)
                    if b == 0 and c:
                        second_tile(2 * stage, c - 1)
                    if b == 1 and stage == 0 and c == 1:
                        stats(1, 0)
                with dve.Fori(0, (NC - 6) // 2) as k:
                    for p in range(2):
                        chunk(p, 2 * k + (at + 4 + p), True)
                if b == 1 and stage == 0:
                    normalise(1, 0, 0)
                    normalise(1, 0, 1)
                for c in range(NC - 2, NC):
                    chunk(c % 2, at + c, b == 0 or c == NC - 2)
                    if b == 0 and c == NC - 2:
                        second_tile(2 * stage, 3)

            def add_ffn(stage, b):
                for n, i in enumerate(Y_ORDER):
                    if n < QT - 1:
                        dve.wait_ge(ffn_y_done, (stage * NB + b) * (QT - 1) + n + 1)
                    else:
                        dve.wait_ge(down_done, (stage * NB + b + 1) * NC)
                    t = b * QT + i
                    dve.scalar_tensor_tensor(x[:, t, :], ffn_y[i][:, :], 0.5, x[:, t, :], ALU.mult,
                                             ALU.add).then_inc(ffn_y_added, 1)

            def ffn_both(stage):
                stats(2 * stage, 1)
                ffn(stage, 0)
                add_ffn(stage, 0)
                ffn(stage, 1)

            def project(g, b, r):
                R = 2 * NR * g + (NR * b + r)
                src = pj_bank[(b * NR + r) % 2]
                if r < NW - 1:
                    dve.wait_ge(pj_hi_done, (2 * (NW - 1)) * g + ((NW - 1) * b + r + 1))
                if r == 0:
                    dve.tensor_tensor(k_lo[b][:, :], src[:, :], f(k_hi[b][:, :]), ALU.subtract).then_inc(pj_read, 1)
                elif r < NW - 1:
                    scale = qscales[:, ds(GH * g + (r - 1), 1)] if not isinstance(g, int) else qscales[:, GH * g + r - 1:GH * g + r]
                    dve.scalar_tensor_tensor(q_lo[b][:, r - 1, :], src[:, :], scale, f(q_hi[b][:, r - 1, :]),
                                             ALU.mult, ALU.subtract).then_inc(pj_read, 1)
                else:
                    j = 2 * (r - NW + 1)
                    V = 2 * NB * g + (2 * b + r - NW + 1)
                    halves = src[:, :].rearrange("p (j a n) -> p j a n", j=2, a=2)
                    dve.wait_ge(v_part_done, V + 1)
                    if not (isinstance(V, int) and V == 0):
                        dve.wait_ge(v_split, V)
                    dve.tensor_tensor(v_sum[:, :, :], halves[:, :, 0, :], v_part[:, :, :], ALU.add).then_inc(pj_read, 1)
                    dve.wait_ge(v_hi_done, V + 1)
                    dve.tensor_tensor(v_lo[b][:, j:j + 2, :], v_sum[:, :, :], f(v_hi[b][:, j:j + 2, :]),
                                      ALU.subtract).then_inc(v_split, 1)

            def add_out(g, b, i):
                Y = NB * QT * g + (QT * b + QT - 1 - i)
                dve.wait_ge(y_done, Y + 1)
                dve.wait_ge(y_free, Y + 1)
                t = b * QT + i
                dve.tensor_tensor(x[:, t, :], x[:, t, :], y_bank[:, :], ALU.add).then_inc(y_free, 1)

            def fill(kind, g, b, arg):
                if kind == "proj":
                    project(g, b, arg)
                elif kind == "out":
                    add_out(g, b, arg)
                elif kind == "stats":
                    stats(2, 0)
                elif kind == "norm":
                    normalise(2, 0, 0)
                    normalise(2, 0, 1)
                    d_low(0, 2 * NC + 1)
                elif kind == "turn":
                    weigh(2, 0, arg)
                    if arg:
                        n_low(2, 0, arg - 1)
                    if 1 <= arg <= 2:
                        normalise(2, 0, arg + 1)
                elif kind == "gate":
                    n_low(2, 0, 3)

            def bias_max(g, n):
                i, hp = unit(n)[1:]
                u = UNITS * g + n
                w = (i + 1) * P
                for h in range(2):
                    dve.wait_ge(s_done, 2 * u + (h + 1))
                    dve.sem_inc(scores_seen, 1)
                    head = 2 * hp + h
                    dve.tensor_tensor_reduce(scores[h][:, 0:w], s_bank[h][:, 0:w], dist[:, SEQ - w:SEQ],
                                             slope_now[:, head:head + 1], 3e38, ALU.add, ALU.min,
                                             neg_max[:, h:h + 1]).then_inc(biased, 1)

            def scale_probs(g, n):
                w = (unit(n)[1] + 1) * P
                u = UNITS * g + n
                dve.wait_ge(exp_done, 2 * u + 2)
                dve.reciprocal(row_inv[:, :], row_sum[:, :]).then_inc(inv_done, 1)
                dve.wait_ge(inv_done, u + 1)
                for h in range(2):
                    ins = dve.tensor_scalar(probs[n % 2][h][:, 0:w], probs[n % 2][h][:, 0:w], row_inv[:, h:h + 1], None, ALU.mult)
                ins.then_inc(p_ready, 1)

            def set_slopes(g):
                src = slopes[:, ds(GH * g, GH)] if not isinstance(g, int) else slopes[:, GH * g:GH * g + GH]
                dve.tensor_copy(slope_now[:, :], src).then_inc(slope_set, 1)
                dve.wait_ge(slope_set, g + 1)

            def slot(g, n):
                b, i, hp = unit(n)
                par = n % 2
                u = UNITS * g + n
                a_fill, b_fill = fillers(g, n)
                for m in range(n_pt(i)):
                    E = PT_BEFORE[UNITS] * g + (PT_BEFORE[n] + m + 1)
                    w = min(2, i + 1 - 2 * m) * 2 * P
                    j = slice(2 * m, 2 * m + w // (2 * P))
                    dve.wait_ge(pt_hi_done, E)
                    dve.tensor_tensor(pt_lo[par][:, j, :], pt_bank[m][:, 0:w], f(pt_hi[par][:, j, :]),
                                      ALU.subtract).then_inc(pt_split, 1)
                if ahead(g, n, 1):
                    scale_probs(*ahead(g, n, 1))
                if ahead(g, n, 2):
                    if n == UNITS - 2:
                        set_slopes(g + 1)
                    bias_max(*ahead(g, n, 2))
                for what in a_fill:
                    fill(*what)
                dve.wait_ge(o_hi_done, u + 1)
                o = slice(2 * hp, 2 * hp + 2)
                dve.tensor_tensor(o_lo[i % 2][:, o, :], o_bank[:, 0:2 * P], f(o_hi[i % 2][:, o, :]),
                                  ALU.subtract).then_inc(o_free, 1)
                for what in b_fill:
                    fill(*what)

            dve.sem_inc(o_free, 1)
            dve.sem_inc(y_free, 1)
            dve.wait_ge(consts_in, 16 * 5)
            stats(0, 0)
            normalise(0, 0, 0)
            normalise(0, 0, 1)
            for i in range(QT):
                weigh(0, 0, i)
                n_low(0, 0, i)
                if i < 2:
                    normalise(0, 0, i + 2)
            d_low(0, 1)
            ffn_both(0)
            n_low(1, 0, 0)
            normalise(1, 0, 2)
            n_low(1, 0, 1)
            normalise(1, 0, 3)
            n_low(1, 0, 2)
            n_low(1, 0, 3)
            add_ffn(0, 1)
            project(0, 0, 0)
            stats(1, 1)
            project(0, 0, 1)
            project(0, 0, 2)
            normalise(1, 1, 0)
            normalise(1, 1, 1)
            project(0, 0, 3)
            project(0, 0, 4)
            n_low(1, 1, 0)
            normalise(1, 1, 2)
            n_low(1, 1, 1)
            normalise(1, 1, 3)
            project(0, 0, 5)
            n_low(1, 1, 2)
            n_low(1, 1, 3)
            project(0, 0, 6)
            set_slopes(0)
            bias_max(0, 0)
            scale_probs(0, 0)
            bias_max(0, 1)
            slot(0, 0)
            with dve.Fori(0, NG - 1) as g:
                for n in range(1, UNITS):
                    slot(g, n)
                slot(g + 1, 0)
            for n in range(1, UNITS):
                slot(NG - 1, n)
            add_out(NG - 1, 1, 0)
            ffn_both(1)
            add_ffn(1, 1)

        @block.tensor
        def _(pe):
            def three(dst, w_hi, w_lo, m_hi, m_lo, first, last):
                pe.matmul(dst, w_hi, m_hi, start=first, stop=False)
                pe.matmul(dst, w_hi, m_lo, start=False, stop=False)
                return pe.matmul(dst, w_lo, m_hi, start=False, stop=last)

            def turn(stage, b, i):
                tile = ln_tile(stage, b, i)
                pe.wait_ge(xn_done, tile + 1)
                if tile >= 2:
                    pe.wait_ge(n_split, tile - 1)
                dst = ln_bank[stage, b][i % 2]
                for k in range(KT):
                    ins = pe.transpose(dst[:, k * P:(k + 1) * P], xn[i % 2][:, k * P:(k + 1) * P], ident[:, :])
                ins.then_inc(xn_turned, 1)

            def half_chunk(b, p, m):
                dst = (ffn_g, ffn_u)[m][p]
                for k in range(KT):
                    ins = three(dst[:, :], gu_hi[p][:, m, k, :], gu_lo[p][:, m, k, :],
                                n_hi[b][:, k, :], n_lo[b][:, k, :], k == 0, k == KT - 1)
                return ins

            def gate_up(b, p, G, tile=None):
                pe.wait_ge(gu_split, G + 1)
                if not isinstance(G, int) or G >= 2:
                    pe.wait_ge(h_done, G - 1)
                if tile:
                    turn(tile[0], 1, tile[1])
                half_chunk(b, p, 0)
                if tile:
                    pe.wait_ge(n_split, ln_tile(tile[0], 1, tile[1]) + 1)
                half_chunk(b, p, 1).then_inc(gu_done, 1)

            def down(p, G, first, last):
                pe.wait_ge(h_split, G + 1)
                pe.wait_ge(d_split, G + 1)
                for i in Y_ORDER:
                    tile = slice(i * P, (i + 1) * P)
                    ins = three(ffn_y[i][:, :], h_hi[p][:, tile], h_lo[p][:, tile], d_hi[p][:, :], d_lo[p][:, :],
                                first, last)
                    if last and i != Y_ORDER[-1]:
                        ins.then_inc(ffn_y_done, 1)
                ins.then_inc(down_done, 1)

            def ffn_both(stage):
                at = stage * NB * NC
                if stage:
                    pe.wait_ge(y_free, 1 + NG * NB * QT)
                else:
                    pe.wait_ge(n_split, QT)
                    gate_up(0, 0, at)
                for b in range(NB):
                    first = at + b * NC
                    for c in range(4):
                        gate_up(b, (c + 1) % 2, first + c + 1, (2 * stage, c - 1) if b == 0 and c else None)
                        if c == 0 and (stage or b):
                            pe.wait_ge(ffn_y_added, (stage * NB + b) * QT)
                        down(c % 2, first + c, c == 0, False)
                    with pe.Fori(0, (NC - 6) // 2) as k:
                        for p in range(2):
                            gate_up(b, 1 - p, 2 * k + (first + 5 + p))
                            down(p, 2 * k + (first + 4 + p), False, False)
                    gate_up(b, 1, first + NC - 1, (2 * stage, 3) if b == 0 else None)
                    down(0, first + NC - 2, False, False)
                    if b == 0:
                        gate_up(1, 0, first + NC)
                    elif stage == 0:
                        turn(1, 0, 0)
                        turn(1, 0, 1)
                    down(1, first + NC - 1, False, True)

            def project(g, b, r):
                R = 2 * NR * g + (NR * b + r)
                dst = pj_bank[(b * NR + r) % 2]
                pe.wait_ge(wq_split, 10 * g + (min(r, NW - 1) + 1))
                if not isinstance(R, int) or R >= 2:
                    pe.wait_ge(pj_read, R - 1)
                if r < NW - 1:
                    for k in range(KT):
                        ins = three(dst[:, :], wq_hi[r][:, k, :], wq_lo[r][:, k, :], n_hi[b][:, k, :],
                                    n_lo[b][:, k, :], k == 0, k == KT - 1)
                else:
                    for j in range(2):
                        tile = slice((2 * (r - NW + 1) + j) * P, (2 * (r - NW + 1) + j + 1) * P)
                        for k in range(KT):
                            both = wv[:, k, :, :]
                            out_ = dst[:, 2 * P * j:2 * P * (j + 1)]
                            pe.matmul(out_, n_hi[b][:, k, tile], both, start=k == 0, stop=False)
                            ins = pe.matmul(out_, n_lo[b][:, k, tile], both, start=False, stop=k == KT - 1)
                ins.then_inc(pj_done, 1)

            def score(g, n):
                b, i, hp = unit(n)
                w = max((i + 1) * P, 2 * P)
                if n % 8 < 2:
                    pe.wait_ge(pj_read, 2 * NR * g + (NR * b + (3 if n % 8 == 0 else 5)))
                u = UNITS * g + n
                if not isinstance(u, int) or u:
                    pe.wait_ge(biased, 2 * u)
                for h in range(2):
                    q = (slice(None), 2 * hp + h, slice(i * P, (i + 1) * P))
                    three(s_bank[h][:, 0:w], q_hi[b][q], q_lo[b][q], k_hi[b][:, 0:w], k_lo[b][:, 0:w],
                          True, True).then_inc(s_done, 1)

            def out_tile(g, b, i):
                Y = NB * QT * g + (QT * b + QT - 1 - i)
                pe.wait_ge(o_free, UNITS * g + (8 * b + 2 * (QT - 1 - i) + 3))
                pe.wait_ge(y_free, Y + 1)
                for h in range(GH):
                    if b == 0 and i == QT - 1:
                        pe.wait_ge(wq_split, 10 * g + (NW + h + 1))
                    ins = three(y_bank[:, :], o_hi[i % 2][:, h, :], o_lo[i % 2][:, h, :], wo_hi[h][:, :],
                                wo_lo[h][:, :], h == 0, h == GH - 1)
                ins.then_inc(y_done, 1)

            def fill(kind, g, b, arg):
                if kind == "proj":
                    project(g, b, arg)
                elif kind == "out":
                    out_tile(g, b, arg)
                elif kind == "turn":
                    turn(2, 0, arg)
                elif kind == "gate":
                    pe.wait_ge(gu_split, 2 * NC + 1)
                    pe.wait_ge(n_split, 5 * QT)
                    half_chunk(0, 0, 0)
                elif kind == "up":
                    half_chunk(0, 0, 1).then_inc(gu_done, 1)

            def slot(g, n):
                b, i, hp = unit(n)
                par = n % 2
                u = UNITS * g + n
                a_fill, b_fill = fillers(g, n)
                pe.wait_ge(p_ready, u + 1)
                for m in range(n_pt(i)):
                    for j in range(2 * m, min(2 * m + 2, i + 1)):
                        for h in range(2):
                            at = (j % 2 * 2 + h) * P
                            ins = pe.transpose(pt_bank[m][:, at:at + P], probs[par][h][:, j * P:(j + 1) * P], ident[:, :])
                    ins.then_inc(pt_done, 1)
                if ahead(g, n, 2):
                    score(*ahead(g, n, 2))
                for what in a_fill:
                    fill(*what)
                if n % 8 == 0:
                    pe.wait_ge(v_split, 2 * NB * g + (2 * b + 2))
                pe.wait_ge(o_free, u + 1)
                for j in range(i + 1):
                    if j % 2 == 0:
                        pe.wait_ge(pt_split, PT_BEFORE[UNITS] * g + (PT_BEFORE[n] + j // 2 + 1))
                    ins = three(o_bank[:, 0:2 * P], v_hi[b][:, j, :], v_lo[b][:, j, :], pt_hi[par][:, j, :],
                                pt_lo[par][:, j, :], j == 0, j == i)
                ins.then_inc(pv_done, 1)
                for what in b_fill:
                    fill(*what)

            pe.wait_ge(consts_in, 16 * 5)
            for i in range(QT):
                turn(0, 0, i)
            ffn_both(0)
            turn(1, 0, 2)
            turn(1, 0, 3)
            pe.wait_ge(n_split, 3 * QT)
            for r in range(4):
                project(0, 0, r)
            turn(1, 1, 0)
            turn(1, 1, 1)
            project(0, 0, 4)
            turn(1, 1, 2)
            turn(1, 1, 3)
            project(0, 0, 5)
            project(0, 0, 6)
            pe.wait_ge(n_split, 4 * QT)
            score(0, 0)
            score(0, 1)
            slot(0, 0)
            with pe.Fori(0, NG - 1) as g:
                for n in range(1, UNITS):
                    slot(g, n)
                slot(g + 1, 0)
            for n in range(1, UNITS):
                slot(NG - 1, n)
            out_tile(NG - 1, 1, 0)
            ffn_both(1)


_INS = ["x", "w_gu", "w_d", "ln_w", "w_qkv", "w_o", "ident", "dist", "slopes", "qscales"]


def kernel(L0_attn_hidden_states, L0_attn_w_qkv, L0_attn_w_o, L0_ffn_ln_w, L0_ffn_gate_w, L0_ffn_up_w, L0_ffn_down_w):
    import numpy as np
    import concourse.bacc as bacc
    from concourse.bass_utils import run_bass_kernel_spmd

    x = np.asarray(L0_attn_hidden_states)
    gate, up, down = (np.asarray(w) for w in (L0_ffn_gate_w, L0_ffn_up_w, L0_ffn_down_w))
    cols = [w.reshape(NC, P, KT, P).transpose(0, 3, 2, 1).reshape(NC, P, KT * P) for w in (gate, up)]
    w_gu = np.ascontiguousarray(np.concatenate(cols, axis=2))
    w_d = np.ascontiguousarray(down.T.reshape(NC, P, D))
    ln_w = np.ascontiguousarray(np.asarray(L0_ffn_ln_w).reshape(KT, P).T)
    wqkv = np.asarray(L0_attn_w_qkv).reshape(KT, P, NG * (GH + 2), P).transpose(2, 1, 0, 3).reshape(-1, P, D)
    nq = NG * GH
    order = [c for g in range(NG) for c in [nq + g] + [GH * g + h for h in range(GH)] + [nq + NG + g]]
    w_qkv = np.ascontiguousarray(wqkv[order])
    w_o = np.ascontiguousarray(np.asarray(L0_attn_w_o).reshape(NG * GH, P, D))
    ident = np.eye(P, dtype=np.float32)
    rel = np.arange(P)[:, None] + (SEQ - P) - np.arange(SEQ)[None, :]
    dist = np.where(rel >= 0, np.sqrt(np.maximum(rel, 0)), MASKED).astype(np.float32)
    slope = (2.0 ** (-8.0 / nq)) ** np.arange(1, nq + 1)
    slopes = np.ascontiguousarray(np.broadcast_to(slope.astype(np.float32), (P, nq)))
    qscales = np.ascontiguousarray(np.broadcast_to((-SCALE / slope).astype(np.float32), (P, nq)))
    arrays = dict(zip(_INS, (x.reshape(-1, D), w_gu, w_d, ln_w, w_qkv, w_o, ident, dist, slopes, qscales)))

    nc = bacc.Bacc("TRN2", target_bir_lowering=False, num_devices=1)
    args = [nc.dram_tensor(f"{n}_dram", arrays[n].shape, F32, kind="ExternalInput").ap() for n in _INS]
    args.append(nc.dram_tensor("out_dram", [NB * SEQ, D], F32, kind="ExternalOutput").ap())
    macaron_kernel(nc, *args)
    r = run_bass_kernel_spmd(nc, [{f"{n}_dram": arrays[n] for n in _INS}], core_ids=[0])
    return r.results[0]["out_dram"].reshape(x.shape)
```

```python
from contextlib import ExitStack

import concourse.bass as bass
from concourse import mybir

F32 = mybir.dt.float32
F32R = mybir.dt.float32r
ALU = mybir.AluOpType
ACT = mybir.ActivationFunctionType

P = 128
D = 512
KT = D // P
SEQ = 512
NB = 2
QT = SEQ // P
INNER = 1792
NC = INNER // P
NG = 8
GH = 4
EPS = 1e-5
SCALE = float(P) ** -0.5
MASKED = 1e37

PAIRS = NG // 2
STEPS = 2 * NB
KQ = 1 + GH
VR = 2
ROUNDS = (KQ + VR, KQ + VR, KQ, KQ)
ROUND_AT = tuple(sum(ROUNDS[:step]) for step in range(STEPS))
PAIR_ROUNDS = sum(ROUNDS)
CHUNKS = [("proj", 0, r) for r in range(KQ)] + [("values", 0, 0), ("values", 0, 1)] + [("out", 0, h) for h in range(GH)]
CHUNKS += [("proj", 1, r) for r in range(KQ)] + [("out", 1, h) for h in range(GH)]
PAIR_CHUNKS = len(CHUNKS)
QKV_CHUNKS = 2 * KQ + 2
Y_ORDER = (2, 3, 0, 1)
RAWQ = 4
UNITS = STEPS * 8
ds = bass.ds


def macaron_kernel(nc, x_in, w_gu, w_d, ln_w, w_qkv, w_o, ident_in, dist_in, slope_in, qscale_in, out):
    ctx = ExitStack()
    with ctx:
        def sem(name):
            return ctx.enter_context(nc.semaphore(name))

        base = (nc.sbuf_base + 31) // 32 * 32
        arena_bytes = (nc.sbuf_bytes_remaining - 64) // 32 * 32
        ctx.enter_context(nc.sbuf_tensor("arena", [P, arena_bytes], mybir.dt.uint8))
        cursor = [base]

        def place(name, shape, dt, at=None):
            size = 4
            for n in shape[1:]:
                size *= n
            where = cursor[0] if at is None else at
            if at is None:
                cursor[0] += (size + 31) // 32 * 32
                assert cursor[0] <= base + arena_bytes, (name, cursor[0] - base, arena_bytes)
            return nc.alloc_sbuf_tensor_at(name, shape, dt, offset=where)

        x = place("x", [P, NB * QT, D], F32)
        n_hi = [place(f"n_hi{b}", [P, KT, SEQ], F32R) for b in range(NB)]
        n_lo = [place(f"n_lo{b}", [P, KT, SEQ], F32R) for b in range(NB)]
        ident = place("ident", [P, P], F32)
        dist = place("dist", [P, SEQ], F32)
        slopes = place("slopes", [P, NG * GH], F32)
        qscales = place("qscales", [P, NG * GH], F32)
        slope_now = place("slope_now", [P, GH], F32)
        qscale_now = place("qscale_now", [P, GH], F32)
        lnw = place("lnw", [P, D], F32)
        stat6 = place("stat6", [P, QT, 6], F32)
        moments = [place(f"moments{b}", [P, QT, 2], F32) for b in range(NB)]
        half_power = place("half_power", [P, QT], F32)
        spread = place("spread", [P, QT], F32)
        rstd_of = [place(f"rstd_of{b}", [P, QT], F32) for b in range(NB)]
        neg_max = place("neg_max", [P, 2], F32)
        row_sum = place("row_sum", [P, 2], F32)
        row_inv = place("row_inv", [P, 2], F32)
        xn = [place(f"xn{n}", [P, D], F32) for n in range(2)]
        xc_at = cursor[0]
        xc = [place(f"xc{n}", [P, D], F32) for n in range(2)]
        raw_at = cursor[0]
        raw_gu = [place(f"raw_gu{p}", [P, 2 * KT * P], F32) for p in range(2)]
        raw_d = [place(f"raw_d{p}", [P, D], F32) for p in range(2)]
        raw_q = [place(f"raw_q{p}", [P, D], F32) for p in range(RAWQ)]
        wo_hi = [place(f"wo_hi{h}", [P, D], F32R) for h in range(GH)]
        wo_lo = [place(f"wo_lo{h}", [P, D], F32R) for h in range(GH)]

        w_at = cursor[0]
        gu_hi = [place(f"gu_hi{p}", [P, 2, KT, P], F32R) for p in range(2)]
        gu_lo = [place(f"gu_lo{p}", [P, 2, KT, P], F32R) for p in range(2)]
        d_hi = [place(f"d_hi{p}", [P, D], F32R) for p in range(2)]
        d_lo = [place(f"d_lo{p}", [P, D], F32R) for p in range(2)]
        chunk = 4 * KT * P
        wq_hi = [place(f"wq_hi{r}", [P, KT, P], F32R, w_at + 2 * r * chunk) for r in range(5)]
        wq_lo = [place(f"wq_lo{r}", [P, KT, P], F32R, w_at + (2 * r + 1) * chunk) for r in range(5)]
        wv_hi = place("wv_hi", [P, KT, 2, P], F32R, w_at + 10 * chunk)
        wv_lo = place("wv_lo", [P, KT, 2, P], F32R, raw_at + 4 * chunk)

        h_at = cursor[0]
        pt_hi = [place(f"pt_hi{p}", [P, QT, 2 * P], F32R) for p in range(2)]
        pt_lo = [place(f"pt_lo{p}", [P, QT, 2 * P], F32R) for p in range(2)]
        row = 4 * SEQ
        silu = [place(f"silu{p}", [P, SEQ], F32, h_at + p * row) for p in range(2)]
        hf = [place(f"hf{p}", [P, SEQ], F32, h_at + (2 + p) * row) for p in range(2)]
        h_hi = [place(f"h_hi{p}", [P, SEQ], F32R, h_at + (4 + p) * row) for p in range(2)]
        h_lo = [place(f"h_lo{p}", [P, SEQ], F32R, h_at + (6 + p) * row) for p in range(2)]

        q_hi = [place(f"q_hi{b}", [P, GH, SEQ], F32R) for b in range(NB)]
        q_lo = [place(f"q_lo{b}", [P, GH, SEQ], F32R) for b in range(NB)]
        k_hi = [place(f"k_hi{b}", [P, SEQ], F32R) for b in range(NB)]
        k_lo = [place(f"k_lo{b}", [P, SEQ], F32R) for b in range(NB)]
        first_kq = [place("first_kq0", [P, KQ, P], F32, xc_at), place("first_kq1", [P, KQ, P], F32)]
        v_hi = [place("v_hi0", [P, QT, 2, P], F32R, raw_at), place("v_hi1", [P, QT, 2, P], F32R)]
        v_lo = [place("v_lo0", [P, QT, 2, P], F32R, raw_at + 2 * chunk), place("v_lo1", [P, QT, 2, P], F32R)]
        scores = [place(f"scores{h}", [P, SEQ], F32) for h in range(2)]
        probs = [[place(f"probs{p}{h}", [P, SEQ], F32) for h in range(2)] for p in range(2)]
        o_hi = [place(f"o_hi{p}", [P, GH, P], F32R) for p in range(2)]
        o_lo = [place(f"o_lo{p}", [P, GH, P], F32R) for p in range(2)]

        bank = [ctx.enter_context(nc.psum_tensor(f"bank{n}", [P, 512], F32)) for n in range(8)]
        ffn_y = bank[0:4]
        ffn_g, ffn_u = [bank[4], bank[5]], [bank[6], bank[7]]
        s_bank, pt_bank, o_bank, y_bank = bank[0:2], bank[2:4], bank[5], bank[7]
        pj_bank = [bank[4], bank[6]]
        ln_bank = {(0, 0): bank[0:2], (0, 1): ffn_u, (1, 0): [bank[4], bank[6], bank[5], bank[7]],
                   (1, 1): [bank[5], bank[7]], (2, 0): [bank[4], bank[6]], (2, 1): ffn_u}

        first_consts_in = sem("first_consts_in")
        first_gate_split = sem("first_gate_split")
        table_loaded = sem("table_loaded")
        tables_in = sem("tables_in")
        x_in_sem = [sem(f"x_in{i}") for i in range(QT + 1)]
        gu_in = [sem(f"gu_in{p}") for p in range(2)]
        d_in = [sem(f"d_in{p}") for p in range(2)]
        q_in = [sem(f"q_in{p}") for p in range(RAWQ)]
        out_written = sem("out_written")
        stat_done, moments_done, power_set, spread_done, rstd_done = (sem(n) for n in ("stat_done", "moments_done", "power_set", "spread_done", "rstd_done"))
        xc_done, xn_done, xn_turned, n_hi_done, n_split = (sem(n) for n in ("xc_done", "xn_done", "xn_turned", "n_hi_done", "n_split"))
        gu_hi_done, gu_split, d_hi_done, d_split = (sem(n) for n in ("gu_hi_done", "gu_split", "d_hi_done", "d_split"))
        gu_done, silu_done, h_done, h_hi_done, h_split = (sem(n) for n in ("gu_done", "silu_done", "h_done", "h_hi_done", "h_split"))
        down_done, ffn_y_done, ffn_y_added = (sem(n) for n in ("down_done", "ffn_y_done", "ffn_y_added"))
        wq_hi_done, wq_split = (sem(n) for n in ("wq_hi_done", "wq_split"))
        pj_done, pj_hi_done, pj_read = (sem(n) for n in ("pj_done", "pj_hi_done", "pj_read"))
        qscale_set = sem("qscale_set")
        slope_set, s_done, biased, exp_done, inv_done, p_ready = (sem(n) for n in ("slope_set", "s_done", "biased", "exp_done", "inv_done", "p_ready"))
        pt_done, pt_hi_done, pt_split = (sem(n) for n in ("pt_done", "pt_hi_done", "pt_split"))
        pv_done, o_hi_done, o_free = (sem(n) for n in ("pv_done", "o_hi_done", "o_free"))
        scores_seen, chunk_begun = (sem(n) for n in ("scores_seen", "chunk_begun"))
        y_done, y_free = (sem(n) for n in ("y_done", "y_free"))

        f = lambda t: t.bitcast(F32)

        def ln_tile(stage, b, n):
            return (stage * NB + b) * QT + n

        def ln_index(stage, b, n):
            return QT - 1 - n if (stage, b) == (2, 0) else n

        def ln_src(stage, b, n):
            if (stage, b) == (2, 0):
                return ln_bank[stage, b][min(n, 1)]
            return ln_bank[stage, b][n % len(ln_bank[stage, b])]

        def unit(n):
            return n // 8 % 2, QT - 1 - n % 8 // 2, n % 2

        def n_pt(i):
            return (i + 2) // 2

        def head_column(table, pair, e, head, n):
            if isinstance(pair, int):
                return table[:, GH * (2 * pair + e) + head:GH * (2 * pair + e) + head + n]
            return table[:, ds(2 * GH * pair + (GH * e + head), n)]

        PT_BEFORE = [sum(n_pt(unit(m)[1]) for m in range(n)) for n in range(UNITS + 1)]
        WITH_V = {0: (["proj 0", "late 0"], []), 1: (["proj 1"], []), 2: (["proj 2"], ["out 3"]),
                  3: (["proj 3"], []), 4: (["proj 4"], ["out 2"]), 5: (["proj 5"], []),
                  6: (["proj 6"], []), 7: (["out 1"], [])}
        NO_V = {0: (["late 0"], []), 1: (["proj 0"], []), 2: (["proj 1"], ["out 3"]),
                3: (["proj 2"], []), 4: (["proj 3"], []), 5: (["proj 4"], []),
                6: (["out 2"], []), 7: (["out 1"], [])}
        LAST = {0: (["late 0"], ["weights 0", "turn 0", "stats 0"]), 1: (["turn 1"], []),
                2: (["turn 2", "out 3"], ["gate 1", "turn 3", "weights 1"]), 3: (["gate 0"], []),
                4: (["up 1"], []), 5: (["out 2"], []), 6: (["up 0"], []), 7: (["out 1"], [])}
        BEFORE_LAST = dict(NO_V)
        BEFORE_LAST[6] = (["out 2"], ["stats 2"])
        BEFORE_LAST[7] = (["out 1"], ["stats 1"])
        FILL = (WITH_V, NO_V, NO_V, WITH_V)

        def ahead(pair, n, by):
            if n + by < UNITS:
                return pair, n + by
            return None if isinstance(pair, int) and pair == PAIRS - 1 else (pair + 1, n + by - UNITS)

        def fillers(pair, n):
            step = n // 8
            last = isinstance(pair, int) and pair == PAIRS - 1 and step >= STEPS - 2

            def full(what):
                kind, arg = what.split()
                if kind == "late":
                    kind = "out"
                    if step == 0 and isinstance(pair, int) and pair == 0:
                        return ("none", 0, 0, 0)
                    return (kind, pair, step - 1, int(arg)) if step else (kind, pair - 1, STEPS - 1, int(arg))
                if kind == "proj":
                    return (kind, pair, step + 1, int(arg)) if step < STEPS - 1 else (kind, pair + 1, 0, int(arg))
                return kind, pair, step, int(arg)

            before, after = ((BEFORE_LAST, LAST)[step - 2] if last else FILL[step])[n % 8]
            return [full(w) for w in before], [full(w) for w in after]

        block = ctx.enter_context(nc.Block())

        @block.sync
        def _(sp):
            x_rows = x_in.rearrange("(t p) d -> p t d", p=P)
            out_rows = out.rearrange("(t p) d -> p t d", p=P)

            def load_gu(c, parity, before):
                sp.wait_ge(gu_split, before)
                sp.dma_start(raw_gu[parity][:, :], w_gu[c]).then_inc(gu_in[parity], 16)

            def load_d(c, parity, before):
                sp.wait_ge(d_split, before)
                sp.dma_start(raw_d[parity][:, :], w_d[c]).then_inc(d_in[parity], 16)

            def load_ffn_first(stage):
                for c in range(2):
                    if stage == 0:
                        if c:
                            sp.dma_start(raw_gu[c][:, :], w_gu[c]).then_inc(gu_in[c], 16)
                        sp.dma_start(raw_d[c][:, :], w_d[c]).then_inc(d_in[c], 16)
                    else:
                        load_gu(c, c, 2 * NC * stage - 1 + c)
                        load_d(c, c, 2 * NC * stage - 1 + c)

            def load_ffn_rest(stage):
                for h in range(NB):
                    first = 2 if h == 0 else 0
                    at = (stage * NB + h) * NC
                    with sp.Fori(0, (NC - first) // 2) as k:
                        for p in range(2):
                            c = 2 * k + (first + p)
                            for src, dst, done, s in ((w_gu, raw_gu, gu_split, gu_in), (w_d, raw_d, d_split, d_in)):
                                sp.wait_ge(done, c + (at - 1))
                                sp.dma_start(dst[p][:, :], src[ds(c, 1)].rearrange("a p n -> (a p) n")).then_inc(s[p], 16)

            def load_pair(pair):
                for c, (kind, e, k) in enumerate(CHUNKS):
                    w, per_pair = (w_o, 2 * GH) if kind == "out" else (w_qkv, QKV_CHUNKS)
                    at = GH * e + k if kind == "out" else (KQ + 2) * e + k + KQ * (kind == "values")
                    if isinstance(pair, int):
                        if PAIR_CHUNKS * pair + c >= RAWQ:
                            sp.wait_ge(wq_split, PAIR_CHUNKS * pair + c - RAWQ + 1)
                        src = w[per_pair * pair + at]
                    else:
                        sp.wait_ge(wq_split, PAIR_CHUNKS * pair + (c - RAWQ + 1))
                        src = w[ds(per_pair * pair + at, 1)].rearrange("a p n -> (a p) n")
                    sp.dma_start(raw_q[c % RAWQ][:, :], src).then_inc(q_in[c % RAWQ], 16)

            for i in range(QT):
                sp.dma_start(x[:, i, :], x_rows[:, i, :]).then_inc(x_in_sem[i], 16)
                if i == 1:
                    sp.dma_start(raw_gu[0][:, :], w_gu[0]).then_inc(gu_in[0], 16)
            load_ffn_first(0)
            for dst, src in ((dist, dist_in), (slopes, slope_in), (qscales, qscale_in)):
                sp.dma_start(dst[:, :], src).then_inc(tables_in, 16)
            sp.dma_start(x[:, QT:, :], x_rows[:, QT:, :]).then_inc(x_in_sem[QT], 16)
            load_ffn_rest(0)
            load_pair(0)
            with sp.Fori(1, PAIRS) as pair:
                load_pair(pair)
            sp.wait_ge(pj_done, PAIR_ROUNDS * (PAIRS - 1) + ROUND_AT[2])
            sp.wait_ge(pv_done, UNITS * PAIRS - 8)
            load_ffn_first(1)
            load_ffn_rest(1)
            for b in range(NB):
                for n, i in enumerate(Y_ORDER):
                    sp.wait_ge(ffn_y_added, (NB + b) * QT + n + 1)
                    t = b * QT + i
                    sp.dma_start(out_rows[:, t, :], x[:, t, :]).then_inc(out_written, 16)
            sp.wait_ge(out_written, 16 * NB * QT)

        @block.gpsimd
        def _(pool):
            def rstd(stage, b, tiles, done):
                n = tiles.stop - tiles.start
                count = ln_tile(stage, b, done) + n
                pool.wait_ge(moments_done, count)
                mul, add = (1.0, EPS) if stage == 1 else (1.0 + EPS, EPS * EPS)
                pool.tensor_scalar(spread[:, tiles], moments[b][:, tiles, 1], mul, add, ALU.mult, ALU.add).then_inc(spread_done, n)
                pool.wait_ge(spread_done, count)
                pool.tensor_tensor(rstd_of[b][:, tiles], spread[:, tiles], half_power[:, tiles], ALU.pow).then_inc(rstd_done, n)

            def normalise(n):
                tile, i = ln_tile(2, 0, n), ln_index(2, 0, n)
                pool.wait_ge(rstd_done, tile + 1)
                pool.wait_ge(s_done, 2 * (UNITS * PAIRS - 8))
                pool.tensor_scalar(xc[n % 2][:, :], x[:, i, :], moments[0][:, i, 0:1], rstd_of[0][:, i:i + 1],
                                   ALU.subtract, ALU.mult).then_inc(xc_done, 1)
                pool.wait_ge(xn_turned, tile - 1)
                pool.wait_ge(xc_done, NB * QT + n + 1)
                pool.tensor_tensor(xn[n % 2][:, :], xc[n % 2][:, :], lnw[:, :], ALU.mult).then_inc(xn_done, 1)

            def first_gu_low():
                pool.wait_ge(gu_hi_done, 1)
                half = KT * P
                pool.tensor_tensor(gu_lo[0][:, 0, :, :], raw_gu[0][:, 0:half], f(gu_hi[0][:, 0, :, :]),
                                   ALU.subtract).then_inc(first_gate_split, 1)
                pool.tensor_tensor(gu_lo[0][:, 1, :, :], raw_gu[0][:, half:2 * half], f(gu_hi[0][:, 1, :, :]),
                                   ALU.subtract).then_inc(gu_split, 1)

            def gu_low(p, count):
                pool.wait_ge(gu_hi_done, count)
                pool.tensor_tensor(gu_lo[p][:, :, :, :], raw_gu[p][:, :], f(gu_hi[p][:, :, :, :]),
                                   ALU.subtract).then_inc(gu_split, 1)

            def ffn(stage):
                at = stage * NB * NC
                with pool.Fori(0, (2 * NC - 4) // 2) as k:
                    for p in range(2):
                        gu_low(p, 2 * k + (at + 2 + p + 1))
                if stage == 0:
                    rstd(1, 0, slice(0, QT), 0)
                for p in range(2):
                    gu_low(p, at + 2 * NC - 2 + p + 1)

            def split_pair(pair):
                first = isinstance(pair, int)
                for c, (kind, e, k) in enumerate(CHUNKS):
                    pool.wait_ge(q_in[c % RAWQ], 16 * (PAIR_CHUNKS // RAWQ * pair + (c // RAWQ + 1)))
                    if first and c == 0:
                        pool.wait_ge(gu_done, 2 * NC)
                    if first and c == 4:
                        pool.wait_ge(down_done, 2 * NC)
                    if not first or (e and kind != "values"):
                        if kind == "proj":
                            before = ROUND_AT[1] if e else ROUND_AT[3] - PAIR_ROUNDS
                            pool.wait_ge(pj_done, PAIR_ROUNDS * pair + (before + k + 1))
                        elif kind == "values":
                            pool.wait_ge(pj_done, PAIR_ROUNDS * pair + (ROUND_AT[2] - PAIR_ROUNDS))
                        else:
                            pool.wait_ge(y_done, STEPS * QT * pair + 2 * QT * e)
                        pool.sem_inc(chunk_begun, 1)
                    raw = raw_q[c % RAWQ]
                    if kind == "proj":
                        hi, lo, src = wq_hi[k][:, :, :], wq_lo[k][:, :, :], raw[:, :].rearrange("p (k n) -> p k n", k=KT)
                    elif kind == "values":
                        hi, lo, src = wv_hi[:, :, k, :], wv_lo[:, :, k, :], raw[:, :].rearrange("p (k n) -> p k n", k=KT)
                    else:
                        hi, lo, src = wo_hi[k][:, :], wo_lo[k][:, :], raw[:, :]
                    pool.tensor_scalar(hi, src, 1.0, 0.0, ALU.mult, ALU.add).then_inc(wq_hi_done, 1)
                    pool.wait_ge(wq_hi_done, PAIR_CHUNKS * pair + (c + 1))
                    pool.tensor_tensor(lo, src, f(hi), ALU.subtract).then_inc(wq_split, 1)
                    if first and c == 3:
                        rstd(1, 1, slice(0, QT), 0)

            pool.memset(half_power[:, :], -0.5).then_inc(power_set, 1)
            pool.wait_ge(power_set, 1)
            rstd(0, 0, slice(0, 1), 0)
            rstd(0, 0, slice(1, 2), 1)
            first_gu_low()
            rstd(0, 0, slice(2, QT), 2)
            gu_low(1, 2)
            rstd(0, 1, slice(0, QT), 0)
            ffn(0)
            split_pair(0)
            with pool.Fori(1, PAIRS) as pair:
                split_pair(pair)
            rstd(2, 0, slice(2, QT), 0)
            normalise(0)
            normalise(1)
            rstd(2, 0, slice(1, 2), 2)
            normalise(2)
            gu_low(0, 2 * NC + 1)
            rstd(2, 0, slice(0, 1), QT - 1)
            normalise(3)
            gu_low(1, 2 * NC + 2)
            rstd(2, 1, slice(0, QT), 0)
            ffn(1)

        @block.scalar
        def _(act):
            def scale(stage, b, n):
                tile, i = ln_tile(stage, b, n), ln_index(stage, b, n)
                act.wait_ge(xc_done, (stage // 2 * NB + b) * QT + n + 1)
                act.wait_ge(rstd_done, tile + 1)
                if tile >= 2:
                    act.wait_ge(xn_turned, tile - 1)
                act.activation(xn[n % 2][:, :], xc[n % 2][:, :], ACT.Copy, scale=rstd_of[b][:, i:i + 1]).then_inc(xn_done, 1)

            def n_high(stage, b, n):
                tile, i = ln_tile(stage, b, n), ln_index(stage, b, n)
                act.wait_ge(xn_turned, tile + 1)
                src = ln_src(stage, b, n)[:, :].rearrange("p (k n) -> p k n", k=KT)
                act.copy(n_hi[b][:, :, i * P:(i + 1) * P], src).then_inc(n_hi_done, 1)

            def gu_high(p, landed, count):
                act.wait_ge(gu_in[p], landed)
                if not isinstance(count, int) or count >= 2:
                    act.wait_ge(gu_done, count - 1)
                act.copy(gu_hi[p][:, :, :, :], raw_gu[p][:, :]).then_inc(gu_hi_done, 1)

            def d_high(p, landed, count):
                act.wait_ge(d_in[p], landed)
                if not isinstance(count, int) or count >= 2:
                    act.wait_ge(down_done, count - 1)
                act.copy(d_hi[p][:, :], raw_d[p][:, :]).then_inc(d_hi_done, 1)

            def chunk(p, G, half_G, more_gu, more_d):
                act.wait_ge(gu_done, G + 1)
                act.activation(silu[p][:, :], ffn_g[p][:, :], ACT.Silu).then_inc(silu_done, 1)
                if more_gu:
                    gu_high(p, 16 * (half_G + 2), G + 2)
                act.wait_ge(h_done, G + 1)
                if not isinstance(G, int) or G >= 2:
                    act.wait_ge(down_done, G - 1)
                act.copy(h_hi[p][:, :], hf[p][:, :]).then_inc(h_hi_done, 1)
                if more_d:
                    d_high(1 - p, 16 * (half_G + p + 1), G + 1)

            def ffn(stage, b):
                at = (stage * NB + b) * NC
                for c in range(4):
                    chunk(c % 2, at + c, (at + c) // 2, True, True)
                    if b == 0 and c == 0:
                        scale(2 * stage, 1, 0)
                        scale(2 * stage, 1, 1)
                    if b == 0 and c:
                        n_high(2 * stage, 1, c - 1)
                        if c <= 2:
                            scale(2 * stage, 1, c + 1)
                with act.Fori(0, (NC - 6) // 2) as k:
                    for p in range(2):
                        chunk(p, 2 * k + (at + 4 + p), k + (at // 2 + 2), True, True)
                for c in range(NC - 2, NC):
                    chunk(c % 2, at + c, (at + c) // 2, b == 0, b == 0 or c == NC - 2)
                    if b == 0 and c == NC - 2:
                        n_high(2 * stage, 1, 3)

            def project(pair, step, r):
                e, b = divmod(step, 2)
                R = PAIR_ROUNDS * pair + (ROUND_AT[step] + r)
                src = pj_bank[(ROUND_AT[step] + r) % 2]
                if r == 0 and not (isinstance(R, int) and R == 0):
                    act.wait_ge(pj_read, R)
                act.wait_ge(pj_done, R + 1)
                if r == 0:
                    act.copy(first_kq[b][:, 0, :], src[:, 0:P])
                    act.copy(k_hi[b][:, :], src[:, :]).then_inc(pj_hi_done, 1)
                    act.copy(qscale_now[:, :], head_column(qscales, pair, e, 0, GH)).then_inc(qscale_set, 1)
                elif r < KQ:
                    if r == 1:
                        act.wait_ge(qscale_set, STEPS * pair + (step + 1))
                    act.activation(first_kq[b][:, r, :], src[:, 0:P], ACT.Copy, scale=qscale_now[:, r - 1:r])
                    act.activation(q_hi[b][:, r - 1, :], src[:, :], ACT.Copy,
                                   scale=qscale_now[:, r - 1:r]).then_inc(pj_hi_done, 1)
                else:
                    j = 2 * (r - KQ)
                    act.copy(v_hi[b][:, j:j + 2, :, :], src[:, :]).then_inc(pj_hi_done, 1)

            def fill(kind, pair, step, arg):
                if kind == "proj":
                    project(pair, step, arg)
                elif kind == "weights":
                    if arg == 0:
                        act.wait_ge(pj_done, PAIRS * PAIR_ROUNDS)
                        gu_high(0, 16 * (NC + 1), NB * NC)
                    else:
                        gu_high(1, 16 * (NC + 1), NB * NC + 1)
                        d_high(0, 16 * (NC + 1), NB * NC)
                elif kind == "turn":
                    n_high(2, 0, arg)

            def exps(pair, n):
                w = (unit(n)[1] + 1) * P
                for h in range(2):
                    act.wait_ge(biased, 2 * UNITS * pair + (2 * n + h + 1))
                    act.activation(probs[n % 2][h][:, 0:w], scores[h][:, 0:w], ACT.Exp, bias=neg_max[:, h:h + 1],
                                   scale=-1.0, accum_out=row_sum[:, h:h + 1]).then_inc(exp_done, 1)

            def slot(pair, n):
                b, i, hp = unit(n)
                par = n % 2
                u = UNITS * pair + n
                a_fill, b_fill = fillers(pair, n)
                for m in range(n_pt(i)):
                    E = PT_BEFORE[UNITS] * pair + (PT_BEFORE[n] + m + 1)
                    w = min(2, i + 1 - 2 * m) * 2 * P
                    act.wait_ge(pt_done, E)
                    act.copy(pt_hi[par][:, 2 * m:2 * m + w // (2 * P), :],
                             pt_bank[m][:, 0:w]).then_inc(pt_hi_done, 1)
                if ahead(pair, n, 2):
                    exps(*ahead(pair, n, 2))
                for what in a_fill:
                    fill(*what)
                act.wait_ge(pv_done, u + 1)
                act.copy(o_hi[i % 2][:, 2 * hp:2 * hp + 2, :], o_bank[:, 0:2 * P]).then_inc(o_hi_done, 1)
                for what in b_fill:
                    fill(*what)

            for dst, src in ((ident, ident_in), (lnw, ln_w)):
                act.dma_start(dst[:, :], src).then_inc(first_consts_in, 16)
            act.wait_ge(power_set, 1)
            act.activation(row_sum[:, :], half_power[:, 0:2], ACT.Silu).then_inc(table_loaded, 1)
            scale(0, 0, 0)
            scale(0, 0, 1)
            gu_high(0, 16, 0)
            n_high(0, 0, 0)
            n_high(0, 0, 1)
            scale(0, 0, 2)
            scale(0, 0, 3)
            gu_high(1, 16, 1)
            n_high(0, 0, 2)
            n_high(0, 0, 3)
            d_high(0, 16, 0)
            ffn(0, 0)
            ffn(0, 1)
            for i in range(QT):
                n_high(1, 0, i)
            act.wait_ge(tables_in, 16 * 3)
            for r in range(KQ):
                project(0, 0, r)
            n_high(1, 1, 0)
            n_high(1, 1, 1)
            exps(0, 0)
            project(0, 0, 5)
            n_high(1, 1, 2)
            n_high(1, 1, 3)
            exps(0, 1)
            project(0, 0, 6)
            slot(0, 0)
            with act.Fori(0, PAIRS - 1) as pair:
                for n in range(1, UNITS):
                    slot(pair, n)
                slot(pair + 1, 0)
            for n in range(1, UNITS):
                slot(PAIRS - 1, n)
            ffn(1, 0)
            ffn(1, 1)

        @block.vector
        def _(dve):
            def stats(stage, b, tiles, done=0):
                at = ln_tile(stage, b, done)
                if (stage, b) == (0, 1):
                    dve.wait_ge(x_in_sem[QT], 16)
                elif stage == 1:
                    dve.wait_ge(ffn_y_added, (b + 1) * QT)
                elif (stage, b) == (2, 1):
                    dve.wait_ge(y_free, 1 + NG * NB * QT)
                elif stage == 2:
                    dve.wait_ge(y_free, 1 + (NG * NB - 1) * QT - tiles[0])
                if at:
                    dve.wait_ge(moments_done, at)
                for i in tiles:
                    if (stage, b) == (0, 0):
                        dve.wait_ge(x_in_sem[i], 16)
                    dve.bn_stats(stat6[:, i, :], x[:, b * QT + i, :]).then_inc(stat_done, 1)
                dve.wait_ge(stat_done, at + len(tiles))
                for i in tiles:
                    dve.bn_aggr(moments[b][:, i, :], stat6[:, i, :]).then_inc(moments_done, 1)

            def centre(stage, b, n):
                tile, i = ln_tile(stage, b, n), ln_index(stage, b, n)
                dve.wait_ge(moments_done, tile + 1)
                if tile >= 2:
                    dve.wait_ge(xn_done, tile - 1)
                dve.scalar_tensor_tensor(xc[n % 2][:, :], x[:, b * QT + i, :], moments[b][:, i, 0:1], lnw[:, :],
                                         ALU.subtract, ALU.mult).then_inc(xc_done, 1)

            def normalise(b, n):
                tile = ln_tile(1, b, n)
                dve.wait_ge(rstd_done, tile + 1)
                dve.wait_ge(xn_turned, tile - 1)
                dve.tensor_scalar(xn[n % 2][:, :], x[:, b * QT + n, :], moments[b][:, n, 0:1],
                                  rstd_of[b][:, n:n + 1], ALU.subtract, ALU.mult).then_inc(xn_done, 1)

            def n_low(stage, b, n):
                tile, i = ln_tile(stage, b, n), ln_index(stage, b, n)
                src = ln_src(stage, b, n)[:, :].rearrange("p (k n) -> p k n", k=KT)
                dve.wait_ge(n_hi_done, tile + 1)
                dve.tensor_tensor(n_lo[b][:, :, i * P:(i + 1) * P], src, f(n_hi[b][:, :, i * P:(i + 1) * P]),
                                  ALU.subtract).then_inc(n_split, 1)

            def d_low(p, count):
                dve.wait_ge(d_hi_done, count)
                dve.tensor_tensor(d_lo[p][:, :], raw_d[p][:, :], f(d_hi[p][:, :]), ALU.subtract).then_inc(d_split, 1)

            def chunk(p, G, more_d):
                dve.wait_ge(silu_done, G + 1)
                if not isinstance(G, int) or G >= 2:
                    dve.wait_ge(h_split, G - 1)
                dve.tensor_tensor(hf[p][:, :], ffn_u[p][:, :], silu[p][:, :], ALU.mult).then_inc(h_done, 1)
                dve.wait_ge(h_hi_done, G + 1)
                dve.tensor_tensor(h_lo[p][:, :], hf[p][:, :], f(h_hi[p][:, :]), ALU.subtract).then_inc(h_split, 1)
                if more_d:
                    d_low(1 - p, G + 2)

            def second_tile(stage, i):
                n_low(stage, 1, i)
                if i < 2:
                    centre(stage, 1, i + 2)

            def ffn(stage, b):
                at = (stage * NB + b) * NC
                for c in range(4):
                    chunk(c % 2, at + c, True)
                    if b == 0 and c == 0:
                        centre(2 * stage, 1, 0)
                        centre(2 * stage, 1, 1)
                    if b == 0 and c:
                        second_tile(2 * stage, c - 1)
                    if b == 1 and stage == 0 and c == 1:
                        stats(1, 0, range(QT))
                with dve.Fori(0, (NC - 6) // 2) as k:
                    for p in range(2):
                        chunk(p, 2 * k + (at + 4 + p), True)
                if b == 1 and stage == 0:
                    normalise(0, 0)
                    normalise(0, 1)
                for c in range(NC - 2, NC):
                    chunk(c % 2, at + c, b == 0 or c == NC - 2)
                    if b == 0 and c == NC - 2:
                        second_tile(2 * stage, 3)

            def add_ffn(stage, b):
                for n, i in enumerate(Y_ORDER):
                    if n < QT - 1:
                        dve.wait_ge(ffn_y_done, (stage * NB + b) * (QT - 1) + n + 1)
                    else:
                        dve.wait_ge(down_done, (stage * NB + b + 1) * NC)
                    t = b * QT + i
                    dve.scalar_tensor_tensor(x[:, t, :], ffn_y[i][:, :], 0.5, x[:, t, :], ALU.mult,
                                             ALU.add).then_inc(ffn_y_added, 1)

            def ffn_both(stage):
                stats(2 * stage, 1, range(QT))
                ffn(stage, 0)
                add_ffn(stage, 0)
                ffn(stage, 1)

            def project(pair, step, r):
                e, b = divmod(step, 2)
                src = pj_bank[(ROUND_AT[step] + r) % 2]
                dve.wait_ge(pj_hi_done, PAIR_ROUNDS * pair + (ROUND_AT[step] + r + 1))
                if r == 0:
                    dve.tensor_tensor(k_lo[b][:, :], src[:, :], f(k_hi[b][:, :]), ALU.subtract).then_inc(pj_read, 1)
                elif r < KQ:
                    dve.scalar_tensor_tensor(q_lo[b][:, r - 1, :], src[:, :], qscale_now[:, r - 1:r],
                                             f(q_hi[b][:, r - 1, :]), ALU.mult, ALU.subtract).then_inc(pj_read, 1)
                else:
                    j = 2 * (r - KQ)
                    dve.tensor_tensor(v_lo[b][:, j:j + 2, :, :], src[:, :], f(v_hi[b][:, j:j + 2, :, :]),
                                      ALU.subtract).then_inc(pj_read, 1)

            def add_out(pair, step, i):
                Y = STEPS * QT * pair + (QT * step + QT - 1 - i)
                b = step % 2
                dve.wait_ge(y_done, Y + 1)
                dve.wait_ge(y_free, Y + 1)
                t = b * QT + i
                dve.tensor_tensor(x[:, t, :], x[:, t, :], y_bank[:, :], ALU.add).then_inc(y_free, 1)

            def fill(kind, pair, step, arg):
                if kind == "proj":
                    project(pair, step, arg)
                elif kind == "out":
                    add_out(pair, step, arg)
                elif kind == "stats":
                    if arg == 2:
                        stats(2, 0, [2, 3])
                    else:
                        stats(2, 0, [arg], QT - 1 - arg)
                elif kind == "turn":
                    n_low(2, 0, arg)
                elif kind == "weights":
                    if arg:
                        d_low(0, 2 * NC + 1)

            def bias_max(pair, n):
                i, hp = unit(n)[1:]
                u = UNITS * pair + n
                w = (i + 1) * P
                for h in range(2):
                    dve.wait_ge(s_done, 2 * u + (h + 1))
                    dve.sem_inc(scores_seen, 1)
                    head = 2 * hp + h
                    dve.tensor_tensor_reduce(scores[h][:, 0:w], s_bank[h][:, 0:w], dist[:, SEQ - w:SEQ],
                                             slope_now[:, head:head + 1], 3e38, ALU.add, ALU.min,
                                             neg_max[:, h:h + 1]).then_inc(biased, 1)

            def scale_probs(pair, n):
                w = (unit(n)[1] + 1) * P
                u = UNITS * pair + n
                dve.wait_ge(exp_done, 2 * u + 2)
                dve.reciprocal(row_inv[:, :], row_sum[:, :]).then_inc(inv_done, 1)
                dve.wait_ge(inv_done, u + 1)
                for h in range(2):
                    ins = dve.tensor_scalar(probs[n % 2][h][:, 0:w], probs[n % 2][h][:, 0:w], row_inv[:, h:h + 1], None, ALU.mult)
                ins.then_inc(p_ready, 1)

            def set_slopes(pair, e):
                dve.tensor_copy(slope_now[:, :], head_column(slopes, pair, e, 0, GH)).then_inc(slope_set, 1)
                dve.wait_ge(slope_set, 2 * pair + (e + 1))

            def slot(pair, n):
                b, i, hp = unit(n)
                par = n % 2
                u = UNITS * pair + n
                a_fill, b_fill = fillers(pair, n)
                for m in range(n_pt(i)):
                    E = PT_BEFORE[UNITS] * pair + (PT_BEFORE[n] + m + 1)
                    w = min(2, i + 1 - 2 * m) * 2 * P
                    j = slice(2 * m, 2 * m + w // (2 * P))
                    dve.wait_ge(pt_hi_done, E)
                    dve.tensor_tensor(pt_lo[par][:, j, :], pt_bank[m][:, 0:w], f(pt_hi[par][:, j, :]),
                                      ALU.subtract).then_inc(pt_split, 1)
                if ahead(pair, n, 1):
                    scale_probs(*ahead(pair, n, 1))
                if ahead(pair, n, 2):
                    if n % 16 == 14:
                        set_slopes(*((pair, 1) if n < 16 else (pair + 1, 0)))
                    bias_max(*ahead(pair, n, 2))
                for what in a_fill:
                    fill(*what)
                dve.wait_ge(o_hi_done, u + 1)
                o = slice(2 * hp, 2 * hp + 2)
                dve.tensor_tensor(o_lo[i % 2][:, o, :], o_bank[:, 0:2 * P], f(o_hi[i % 2][:, o, :]),
                                  ALU.subtract).then_inc(o_free, 1)
                for what in b_fill:
                    fill(*what)

            dve.sem_inc(o_free, 1)
            dve.sem_inc(y_free, 1)
            stats(0, 0, [0])
            dve.wait_ge(first_consts_in, 16 * 2)
            centre(0, 0, 0)
            stats(0, 0, [1], 1)
            centre(0, 0, 1)
            stats(0, 0, [2, 3], 2)
            centre(0, 0, 2)
            n_low(0, 0, 0)
            n_low(0, 0, 1)
            centre(0, 0, 3)
            n_low(0, 0, 2)
            n_low(0, 0, 3)
            d_low(0, 1)
            ffn_both(0)
            n_low(1, 0, 0)
            normalise(0, 2)
            n_low(1, 0, 1)
            normalise(0, 3)
            n_low(1, 0, 2)
            n_low(1, 0, 3)
            add_ffn(0, 1)
            project(0, 0, 0)
            stats(1, 1, range(QT))
            project(0, 0, 1)
            project(0, 0, 2)
            normalise(1, 0)
            normalise(1, 1)
            project(0, 0, 3)
            project(0, 0, 4)
            n_low(1, 1, 0)
            normalise(1, 2)
            n_low(1, 1, 1)
            normalise(1, 3)
            dve.wait_ge(tables_in, 16 * 3)
            set_slopes(0, 0)
            bias_max(0, 0)
            project(0, 0, 5)
            n_low(1, 1, 2)
            n_low(1, 1, 3)
            scale_probs(0, 0)
            bias_max(0, 1)
            project(0, 0, 6)
            slot(0, 0)
            with dve.Fori(0, PAIRS - 1) as pair:
                for n in range(1, UNITS):
                    slot(pair, n)
                slot(pair + 1, 0)
            for n in range(1, UNITS):
                slot(PAIRS - 1, n)
            add_out(PAIRS - 1, STEPS - 1, 0)
            ffn_both(1)
            add_ffn(1, 1)

        @block.tensor
        def _(pe):
            def three(dst, w_hi, w_lo, m_hi, m_lo, first, last):
                pe.matmul(dst, w_hi, m_hi, start=first, stop=False)
                pe.matmul(dst, w_hi, m_lo, start=False, stop=False)
                return pe.matmul(dst, w_lo, m_hi, start=False, stop=last)

            def turn(stage, b, n):
                tile = ln_tile(stage, b, n)
                pe.wait_ge(xn_done, tile + 1)
                if tile >= 2:
                    pe.wait_ge(n_split, tile - 1)
                if (stage, b) == (2, 0) and n >= 2:
                    pe.wait_ge(n_split, tile)
                dst = ln_src(stage, b, n)
                for k in range(KT):
                    ins = pe.transpose(dst[:, k * P:(k + 1) * P], xn[n % 2][:, k * P:(k + 1) * P], ident[:, :])
                ins.then_inc(xn_turned, 1)

            def half_chunk(b, p, m, tokens=slice(0, SEQ)):
                dst = (ffn_g, ffn_u)[m][p]
                for k in range(KT):
                    ins = three(dst[:, tokens], gu_hi[p][:, m, k, :], gu_lo[p][:, m, k, :],
                                n_hi[b][:, k, tokens], n_lo[b][:, k, tokens], k == 0, k == KT - 1)
                return ins

            def gate_up(b, p, G, tile=None, after_attention=False):
                pe.wait_ge(gu_split, G + 1)
                if not isinstance(G, int) or G >= 2:
                    pe.wait_ge(h_done, G - 1)
                if tile:
                    turn(tile[0], 1, tile[1])
                half_chunk(b, p, 0)
                if tile:
                    pe.wait_ge(n_split, ln_tile(tile[0], 1, tile[1]) + 1)
                if after_attention:
                    pe.wait_ge(y_free, 1 + NG * NB * QT)
                half_chunk(b, p, 1).then_inc(gu_done, 1)

            def down(p, G, first, last, turns=()):
                pe.wait_ge(h_split, G + 1)
                pe.wait_ge(d_split, G + 1)
                for n, i in enumerate(Y_ORDER):
                    if turns and n in (0, 2):
                        turn(*turns[n])
                        turn(*turns[n + 1])
                    tile = slice(i * P, (i + 1) * P)
                    ins = three(ffn_y[i][:, :], h_hi[p][:, tile], h_lo[p][:, tile], d_hi[p][:, :], d_lo[p][:, :],
                                first, last)
                    if last and i != Y_ORDER[-1]:
                        ins.then_inc(ffn_y_done, 1)
                ins.then_inc(down_done, 1)

            def ffn_both(stage):
                at = stage * NB * NC
                if stage:
                    pe.wait_ge(o_free, 1 + UNITS * PAIRS)
                for b in range(NB):
                    first = at + b * NC
                    for c in range(4):
                        gate_up(b, (c + 1) % 2, first + c + 1, (2 * stage, c - 1) if b == 0 and c else None,
                                stage == 1 and b == 0 and c == 0)
                        if c == 0 and (stage or b):
                            pe.wait_ge(ffn_y_added, (stage * NB + b) * QT)
                        down(c % 2, first + c, c == 0, False)
                    with pe.Fori(0, (NC - 6) // 2) as k:
                        for p in range(2):
                            gate_up(b, 1 - p, 2 * k + (first + 5 + p))
                            down(p, 2 * k + (first + 4 + p), False, False)
                    gate_up(b, 1, first + NC - 1, (2 * stage, 3) if b == 0 else None)
                    down(0, first + NC - 2, False, False)
                    if b == 0:
                        gate_up(1, 0, first + NC)
                    down(1, first + NC - 1, False, True, [(1, 0, n) for n in range(QT)] if (stage, b) == (0, 1) else ())

            def project(pair, step, r):
                e, b = divmod(step, 2)
                R = PAIR_ROUNDS * pair + (ROUND_AT[step] + r)
                dst = pj_bank[(ROUND_AT[step] + r) % 2]
                chunks = (KQ + 2 + GH) * e + (r + 1 if r < KQ else KQ + 2)
                pe.wait_ge(wq_split, PAIR_CHUNKS * pair + chunks)
                if not isinstance(R, int) or R >= 2:
                    pe.wait_ge(pj_read, R - 1)
                if r < KQ:
                    for k in range(KT):
                        ins = three(dst[:, :], wq_hi[r][:, k, :], wq_lo[r][:, k, :], n_hi[b][:, k, :],
                                    n_lo[b][:, k, :], k == 0, k == KT - 1)
                else:
                    for j in range(2):
                        tile = slice((2 * (r - KQ) + j) * P, (2 * (r - KQ) + j + 1) * P)
                        for k in range(KT):
                            ins = three(dst[:, 2 * P * j:2 * P * (j + 1)], n_hi[b][:, k, tile], n_lo[b][:, k, tile],
                                        wv_hi[:, k, :, :], wv_lo[:, k, :, :], k == 0, k == KT - 1)
                ins.then_inc(pj_done, 1)

            def score(pair, n):
                b, i, hp = unit(n)
                w = (i + 1) * P
                if n % 8 < 2:
                    pe.wait_ge(pj_read, PAIR_ROUNDS * pair + (ROUND_AT[n // 8] + (3 if n % 8 == 0 else 5)))
                u = UNITS * pair + n
                if not isinstance(u, int) or u:
                    pe.wait_ge(biased, 2 * u)
                for h in range(2):
                    q = (slice(None), 2 * hp + h, slice(i * P, (i + 1) * P))
                    if i == 0:
                        ins = pe.matmul(s_bank[h][:, 0:w], first_kq[b][:, 1 + 2 * hp + h, :], first_kq[b][:, 0, :],
                                        start=True, stop=True)
                    else:
                        ins = three(s_bank[h][:, 0:w], q_hi[b][q], q_lo[b][q], k_hi[b][:, 0:w], k_lo[b][:, 0:w],
                                    True, True)
                    ins.then_inc(s_done, 1)

            def out_tile(pair, step, i):
                Y = STEPS * QT * pair + (QT * step + QT - 1 - i)
                e, b = divmod(step, 2)
                pe.wait_ge(o_free, UNITS * pair + (8 * step + 2 * (QT - 1 - i) + 3))
                pe.wait_ge(y_free, Y + 1)
                for h in range(GH):
                    if b == 0 and i == QT - 1:
                        first_out = KQ + 2 if e == 0 else PAIR_CHUNKS - GH
                        pe.wait_ge(wq_split, PAIR_CHUNKS * pair + (first_out + h + 1))
                    ins = three(y_bank[:, :], o_hi[i % 2][:, h, :], o_lo[i % 2][:, h, :], wo_hi[h][:, :],
                                wo_lo[h][:, :], h == 0, h == GH - 1)
                ins.then_inc(y_done, 1)

            def fill(kind, pair, step, arg):
                if kind == "proj":
                    project(pair, step, arg)
                elif kind == "out":
                    out_tile(pair, step, arg)
                elif kind == "turn":
                    turn(2, 0, arg)
                elif kind in ("gate", "up"):
                    pe.wait_ge(gu_split, 2 * NC + 1)
                    pe.wait_ge(n_split, ln_tile(2, 0, 2 if arg and kind == "gate" else QT))
                    ins = half_chunk(0, 0, int(kind == "up"), slice(arg * 2 * P, (arg + 1) * 2 * P))
                    if kind == "up" and arg == 0:
                        ins.then_inc(gu_done, 1)

            def slot(pair, n):
                b, i, hp = unit(n)
                par = n % 2
                u = UNITS * pair + n
                a_fill, b_fill = fillers(pair, n)
                pe.wait_ge(p_ready, u + 1)
                for m in range(n_pt(i)):
                    for j in range(2 * m, min(2 * m + 2, i + 1)):
                        for h in range(2):
                            at = (j % 2 * 2 + h) * P
                            ins = pe.transpose(pt_bank[m][:, at:at + P], probs[par][h][:, j * P:(j + 1) * P], ident[:, :])
                    ins.then_inc(pt_done, 1)
                if ahead(pair, n, 2):
                    score(*ahead(pair, n, 2))
                for what in a_fill:
                    fill(*what)
                e = n // 16
                if n % 8 == 0 and e == 0:
                    pe.wait_ge(pj_read, PAIR_ROUNDS * pair + (ROUND_AT[n // 8] + KQ + 2))
                pe.wait_ge(o_free, u + 1)
                for j in range(i + 1):
                    if j % 2 == 0:
                        pe.wait_ge(pt_split, PT_BEFORE[UNITS] * pair + (PT_BEFORE[n] + j // 2 + 1))
                    ins = three(o_bank[:, 0:2 * P], v_hi[b][:, j, e, :], v_lo[b][:, j, e, :], pt_hi[par][:, j, :],
                                pt_lo[par][:, j, :], j == 0, j == i)
                ins.then_inc(pv_done, 1)
                for what in b_fill:
                    fill(*what)

            pe.wait_ge(first_consts_in, 16 * 2)
            turn(0, 0, 0)
            turn(0, 0, 1)
            pe.wait_ge(first_gate_split, 1)
            pe.wait_ge(n_split, 2)
            half_chunk(0, 0, 0, slice(0, 2 * P))
            turn(0, 0, 2)
            turn(0, 0, 3)
            pe.wait_ge(gu_split, 1)
            half_chunk(0, 0, 1, slice(0, 2 * P))
            pe.wait_ge(n_split, QT)
            half_chunk(0, 0, 0, slice(2 * P, SEQ))
            half_chunk(0, 0, 1, slice(2 * P, SEQ)).then_inc(gu_done, 1)
            ffn_both(0)
            pe.wait_ge(n_split, 3 * QT)
            for r in range(KQ):
                project(0, 0, r)
            turn(1, 1, 0)
            turn(1, 1, 1)
            score(0, 0)
            project(0, 0, 5)
            turn(1, 1, 2)
            turn(1, 1, 3)
            score(0, 1)
            project(0, 0, 6)
            pe.wait_ge(n_split, 4 * QT)
            slot(0, 0)
            with pe.Fori(0, PAIRS - 1) as pair:
                for n in range(1, UNITS):
                    slot(pair, n)
                slot(pair + 1, 0)
            for n in range(1, UNITS):
                slot(PAIRS - 1, n)
            out_tile(PAIRS - 1, STEPS - 1, 0)
            ffn_both(1)


_INS = ["x", "w_gu", "w_d", "ln_w", "w_qkv", "w_o", "ident", "dist", "slopes", "qscales"]


def kernel(L0_attn_hidden_states, L0_attn_w_qkv, L0_attn_w_o, L0_ffn_ln_w, L0_ffn_gate_w, L0_ffn_up_w, L0_ffn_down_w):
    import numpy as np
    import concourse.bacc as bacc
    from concourse.bass_utils import run_bass_kernel_spmd

    x = np.asarray(L0_attn_hidden_states)
    gate, up, down = (np.asarray(w) for w in (L0_ffn_gate_w, L0_ffn_up_w, L0_ffn_down_w))
    cols = [w.reshape(NC, P, KT, P).transpose(0, 3, 2, 1).reshape(NC, P, KT * P) for w in (gate, up)]
    w_gu = np.ascontiguousarray(np.concatenate(cols, axis=2))
    w_d = np.ascontiguousarray(down.T.reshape(NC, P, D))
    ln_w = np.ascontiguousarray(np.broadcast_to(np.asarray(L0_ffn_ln_w), (P, D)))
    wqkv = np.asarray(L0_attn_w_qkv).reshape(KT, P, NG * (GH + 2), P).transpose(2, 1, 0, 3).reshape(-1, P, D)
    nq = NG * GH
    key_query = [[nq + g] + [GH * g + h for h in range(GH)] for g in range(NG)]
    order = [c for g in range(0, NG, 2) for c in key_query[g] + [nq + NG + g, nq + NG + g + 1] + key_query[g + 1]]
    w_qkv = np.ascontiguousarray(wqkv[order])
    w_o = np.ascontiguousarray(np.asarray(L0_attn_w_o).reshape(NG * GH, P, D))
    ident = np.eye(P, dtype=np.float32)
    rel = np.arange(P)[:, None] + (SEQ - P) - np.arange(SEQ)[None, :]
    dist = np.where(rel >= 0, np.sqrt(np.maximum(rel, 0)), MASKED).astype(np.float32)
    slope = (2.0 ** (-8.0 / nq)) ** np.arange(1, nq + 1)
    slopes = np.ascontiguousarray(np.broadcast_to(slope.astype(np.float32), (P, nq)))
    qscales = np.ascontiguousarray(np.broadcast_to((-SCALE / slope).astype(np.float32), (P, nq)))
    arrays = dict(zip(_INS, (x.reshape(-1, D), w_gu, w_d, ln_w, w_qkv, w_o, ident, dist, slopes, qscales)))

    nc = bacc.Bacc("TRN2", target_bir_lowering=False, num_devices=1)
    args = [nc.dram_tensor(f"{n}_dram", arrays[n].shape, F32, kind="ExternalInput").ap() for n in _INS]
    args.append(nc.dram_tensor("out_dram", [NB * SEQ, D], F32, kind="ExternalOutput").ap())
    macaron_kernel(nc, *args)
    r = run_bass_kernel_spmd(nc, [{f"{n}_dram": arrays[n] for n in _INS}], core_ids=[0])
    return r.results[0]["out_dram"].reshape(x.shape)
```
